# Optimizing a Trainium2 kernel written in Bass

```python
import numpy as np
import jax
import jax.numpy as jnp

def _softmax(x, axis=-1):
    return jax.nn.softmax(x, axis=axis)
def _gelu(x):
    return jax.nn.gelu(x, approximate=True)
def _silu(x):
    return jax.nn.silu(x)
def _sigmoid(x):
    return jax.nn.sigmoid(x)
def _layernorm(x, axis=-1, eps=1e-5):
    m = jnp.mean(x, axis=axis, keepdims=True)
    v = jnp.var(x, axis=axis, keepdims=True)
    return (x - m) / jnp.sqrt(v + eps)
def _scatter_add(tgt, idx, src, axis=0):
    return tgt.at[idx].add(src)
def _segment_sum(src, seg, n):
    return jax.ops.segment_sum(src, seg, n)

kernel_name = 'mk_conv_preact_d1_conv_nchw192_834165'

def setup_inputs(seed: int = 0):
    np.random.seed(seed)
    _w = jnp.asarray
    def _rec_inputs():
        import jax
        import jax.numpy as jnp
        _gk = jax.random.key(seed)
        x = -0.000357 + 1 * jax.random.normal(jax.random.fold_in(_gk, 1), (32, 192, 56, 56), jnp.float32)
        return x
    x = _rec_inputs()
    def _L0_conv_setup():
        import jax, jax.numpy as jnp
        import numpy as np
        B, CIN, H, W = (32, 192, 56, 56)
        COUT, K, PAD, STRIDE = (192, 3, 1, 1)
        key = jax.random.key(seed)
        k1, k2 = jax.random.split(key, 2)
        x = jax.random.normal(k1, (B, CIN, H, W), dtype=jnp.float32)
        weight = jax.random.normal(k2, (COUT, CIN * K * K), dtype=jnp.float32) * 0.02
        bias = jnp.zeros((COUT,), dtype=jnp.float32)
        return {'x': x, 'weight': weight, 'bias': bias}
    _L0_conv_all = _L0_conv_setup()
    _L0_conv_in = {k: v for k, v in _L0_conv_all.items() if k in ('weight', 'bias', )}
    del _L0_conv_all

    return {
        "x": x,
        "L0_conv_weight": _L0_conv_in["weight"],
        "L0_conv_bias": _L0_conv_in["bias"],
    }

def reference(x, L0_conv_weight, L0_conv_bias):
    import jax
    import jax.numpy as jnp
    def _L0_conv_ref(x, weight, bias):
        import jax, jax.numpy as jnp
        import numpy as np
        B, CIN, H, W = (32, 192, 56, 56)
        COUT, K, PAD, STRIDE = (192, 3, 1, 1)
        xp = jnp.pad(x, ((0, 0), (0, 0), (PAD, PAD), (PAD, PAD)))
        Bn, C, Hp, Wp = xp.shape
        Ho = (Hp - K) // STRIDE + 1
        Wo = (Wp - K) // STRIDE + 1
        patches = jnp.stack([xp[:, :, i:i + Ho * STRIDE:STRIDE, j:j + Wo * STRIDE:STRIDE] for i in range(K) for j in range(K)], axis=2)
        cols = patches.reshape(Bn, C * K * K, Ho * Wo)
        out = jnp.einsum('bkl,ok->bol', cols, weight) + bias[None, :, None]
        return out.reshape(Bn, COUT, Ho, Wo)

    def _gn(v, G=32, eps=1e-5):
        B_, C_, H_, W_ = v.shape
        g = v.reshape(B_, G, C_ // G, H_, W_)
        m = jnp.mean(g, axis=(2, 3, 4), keepdims=True)
        s = jnp.var(g, axis=(2, 3, 4), keepdims=True)
        return ((g - m) / jnp.sqrt(s + eps)).reshape(v.shape)

    def _ln_c(v, eps=1e-6):
        m = jnp.mean(v, axis=1, keepdims=True)
        s = jnp.var(v, axis=1, keepdims=True)
        return (v - m) / jnp.sqrt(s + eps)

    def _ln_t(v, eps=1e-5):
        m = jnp.mean(v, axis=-1, keepdims=True)
        s = jnp.var(v, axis=-1, keepdims=True)
        return (v - m) / jnp.sqrt(s + eps)

    def _to_tokens(v):
        B_, C_, H_, W_ = v.shape
        return v.reshape(B_, C_, H_ * W_).transpose(0, 2, 1)
    def _from_tokens(t, like):
        B_, C_, H_, W_ = like.shape
        return t.transpose(0, 2, 1).reshape(B_, C_, H_, W_)

    x = x + _L0_conv_ref(_gn(x), L0_conv_weight, L0_conv_bias)
    return x


_drawn_inputs = setup_inputs


def setup_inputs(seed=0):
    import zlib

    import numpy as np

    out = dict(_drawn_inputs(seed))
    spreads = {'L0_conv_bias': (0.0, 0.1)}
    factors = {}
    for name, (base, spread) in spreads.items():
        noise = np.random.default_rng([zlib.crc32(name.encode()), seed]).standard_normal(out[name].shape)
        drawn = base * np.exp(spread * noise) if base else spread * noise
        out[name] = jnp.asarray(drawn.astype(out[name].dtype))
    for name, factor in factors.items():
        out[name] = (out[name] * factor).astype(out[name].dtype)
    return out
```

```python
from contextlib import ExitStack

import numpy as np

import concourse.bass as bass
from concourse import mybir

F32 = mybir.dt.float32
F16 = mybir.dt.float16
I32 = mybir.dt.int32
ALU = mybir.AluOpType
ACT = mybir.ActivationFunctionType
AX = mybir.AxisListType

P = 128
IMAGES, CH, H, W = 32, 192, 56, 56
REST = CH - P
GROUPS, EPS = 32, 1e-5
PER_GROUP = CH // GROUPS
KX = 3
TAPS = 9

STEPS = 4
ROWS = H // STEPS
TILES = ROWS // 2
N = TILES * W
WP = W + 2
PAIRS = IMAGES // 2
CHUNKS = 7
CHUNK = H * W // CHUNKS

SLOT = {0: 0, 3: 1, 1: 2, 2: 3}
ORDER = (SLOT[1], SLOT[2], SLOT[0], SLOT[3])

A, B, R = 0, 1, 2
V_SCALE = 64.0
U_SCALE = 8192.0
LEAST = 2.0 ** -100
EXPONENT = 0x7F800000

PROLOGUE = [(R, 0), (A, 0), (B, 0), (R, 1)]
LEAD = len(PROLOGUE)


def group_matrices():
    a = np.arange(P) // PER_GROUP
    r = (P + np.arange(P) % REST) // PER_GROUP
    image = np.arange(P) // REST
    aa = a[:, None] == a[None]
    ra = r[:, None] == a[None]
    ar = a[:, None] == r[None]
    rr = (r[:, None] == r[None]) & (image[:, None] == image[None])
    mats = [aa, ra & (image[:, None] == 0), ra & (image[:, None] == 1),
            ar & (image[None] == 0), ar & (image[None] == 1), rr]
    return (np.stack(mats, axis=1) / PER_GROUP).astype(np.float32)


AA, RA0, RA1, AR0, AR1, RR = range(6)


def preact_conv(nc, x, w_rows, w_cols, bias, matrices, identity, out):
    with ExitStack() as ctx:
        def sb(name, shape, dt=F32):
            return ctx.enter_context(nc.sbuf_tensor(name, shape, dt))

        def sem(name):
            return ctx.enter_context(nc.semaphore(name))

        xt = sb("xt", [P, 2, 3, H, W])
        norm = sb("norm", [P, 2, ROWS + 2, W])
        v = sb("v", [P, 2, 4, TILES, W])
        va = sb("va", [P, 2, 2, 2, 4, TILES, WP], F16)
        vr = sb("vr", [P, 2, 4, TILES, WP], F16)
        st = sb("st", [P, 2, 2, 2, 4, TILES, WP], F16)
        m1 = sb("m1", [P, 2, N])
        even = sb("even", [P, 2, N])
        odd = sb("odd", [P, 2, N])

        ua = sb("ua", [P, 2, 4, KX, CH], F16)
        ur = sb("ur", [P, 4, KX, CH], F16)
        ul = sb("ul", [P, 4, KX, CH], F16)
        us = sb("us", [P, 4, CH], F16)

        mats = sb("mats", [P, 6, P])
        ident = sb("ident", [P, P])
        ones = sb("ones", [P, P])
        biases = sb("biases", [P, 2])
        unscale = sb("unscale", [P, 2])
        minus = sb("minus", [P, 2])
        scales = sb("scales", [P, 6, 2])
        diag = sb("diag", [P, 2, P])
        row_scale = sb("row_scale", [P, CH])

        bn = sb("bn", [P, 3, CHUNKS, 6])
        moments = sb("moments", [P, 3, 2])
        mean = sb("mean", [P, 2, 3])
        rstd = sb("rstd", [P, 2, 3])
        dev = sb("dev", [P, 3])
        spread = sb("spread", [P, 3])
        ve = sb("ve", [P, 3])
        sd = sb("sd", [P, 3])
        r0 = sb("r0", [P, 3])
        r1 = sb("r1", [P, 3])

        flat = xt[:, 1, :, :, :].rearrange("p u h w -> p (u h w)")
        WIDE = TAPS * CH
        wr = [flat[:, i * WIDE:(i + 1) * WIDE] for i in (0, 1)]
        wc = [flat[:, i * WIDE:(i + 1) * WIDE].rearrange("p (i k o) -> p i k o", i=3, k=KX)
              for i in (2, 3)]
        U0 = 4 * WIDE
        FU = 4 * KX * CH
        u = flat[:, U0:U0 + FU].rearrange("p (s k o) -> p s k o", s=4, k=KX)

        ps = ctx.enter_context(nc.psum_tensor("ps", [P, 8, 512], F32))
        STAT = N + 8

        x_loaded = [[sem(f"x_loaded{p}{t}") for t in range(3)] for p in range(2)]
        w_loaded = sem("w_loaded")
        const_loaded = sem("const_loaded")
        cleared = sem("cleared")
        set_dve = sem("set_dve")
        diag_ready = sem("diag_ready")
        spread_out = sem("spread_out")
        weights_ready = sem("weights_ready")
        moments_in = sem("moments_in")
        moments_out = sem("moments_out")
        moments_read = sem("moments_read")
        var_ready = sem("var_ready")
        sd_ready = sem("sd_ready")
        stat_dve = sem("stat_dve")
        rstd_ready = sem("rstd_ready")
        sp_passed = sem("sp_passed")
        dve_passed = sem("dve_passed")
        normed = sem("normed")
        v_ready = sem("v_ready")
        high_ready = sem("high_ready")
        low_ready = [sem(f"low_ready{t}") for t in range(3)]
        stacked = [sem("stacked0"), sem("stacked1")]
        products = sem("products")
        m1_ready = sem("m1_ready")
        halves = sem("halves")
        residual = sem("residual")
        finished = sem("finished")
        y_stored = [sem("y_stored0"), sem("y_stored1")]

        STACK_INC = 8 * 16
        UNIT_INC = [16, 16, 32]
        PAIR_STORED = STEPS * sum(UNIT_INC)
        CREDIT = 16

        def x_rows(img, lo, hi, r0_, r1_):
            return x[img, lo:hi, r0_:r1_, :]

        block = ctx.enter_context(nc.Block())

        @block.sync
        def _(sp):
            def load(first, par):
                for t in (A, B):
                    sp.dma_start(xt[:, par, t], x[bass.ds(first + t, 1), 0:P].rearrange("n c h w -> (n c) h w"))\
                      .then_inc(x_loaded[par][t], 16)
                for i in (0, 1):
                    sp.dma_start(xt[i * REST:(i + 1) * REST, par, R],
                                 x[bass.ds(first + i, 1), P:CH].rearrange("n c h w -> (n c) h w"))\
                      .then_inc(x_loaded[par][R], 16)

            def store(first, par, t, j):
                rows = slice(j * ROWS, (j + 1) * ROWS)
                if t != R:
                    sp.dma_start(out[bass.ds(first + t, 1), 0:P, rows].rearrange("n c h w -> (n c) h w"),
                                 xt[:, par, t, rows]).then_inc(y_stored[par], 16)
                else:
                    for i in (0, 1):
                        sp.dma_start(out[bass.ds(first + i, 1), P:CH, rows].rearrange("n c h w -> (n c) h w"),
                                     xt[i * REST:(i + 1) * REST, par, t, rows]).then_inc(y_stored[par], 16)

            def stack(step, sp_):
                for i in (0, 1):
                    mine = slice(i * REST, (i + 1) * REST)
                    high = vr[mine, 0].rearrange("p s t c -> p (s t c)")
                    low = vr[mine, 1].rearrange("p s t c -> p (s t c)")
                    s1 = st[:, sp_, i, 0].rearrange("p s t c -> p (s t c)")
                    s2 = st[:, sp_, i, 1].rearrange("p s t c -> p (s t c)")
                    L = 4 * TILES * WP
                    sp.dma_start(s1[0:REST], high).then_inc(stacked[sp_], 16)
                    sp.dma_start(s1[REST:P], low).then_inc(stacked[sp_], 16)
                    sp.dma_start(s2[0:REST], high).then_inc(stacked[sp_], 16)
                    sp.dma_start(s2[REST:P, 0:L - 1], high[:, 1:L]).then_inc(stacked[sp_], 16)

            for i in (0, 1):
                sp.dma_start(wr[0] if i == 0 else wr[1][0:REST], w_rows[0:P] if i == 0 else w_rows[P:CH])\
                  .then_inc(w_loaded, 16)
            sp.dma_start(wr[1][REST:P], w_rows[P:CH]).then_inc(w_loaded, 16)
            sp.dma_start(wc[0], w_cols[0:P]).then_inc(w_loaded, 16)
            for i in (0, 1):
                sp.dma_start(wc[1][i * REST:(i + 1) * REST], w_cols[P:CH]).then_inc(w_loaded, 16)
            sp.dma_start(mats[:], matrices).then_inc(const_loaded, 16)
            sp.dma_start(ident[:], identity).then_inc(const_loaded, 16)
            sp.dma_start(biases[:, 0:1], bias[0:P]).then_inc(const_loaded, 16)
            for i in (0, 1):
                sp.dma_start(biases[i * REST:(i + 1) * REST, 1:2], bias[P:CH]).then_inc(const_loaded, 16)
            load(0, 0)
            for par in (0, 1):
                sp.sem_inc(y_stored[par], CREDIT)
            for k in (0, 1):
                sp.wait_ge(low_ready[R], k + 1)
                stack(k, k % 2)
            sp.wait_ge(weights_ready, 1)

            def body(m, last=False):
                for par in (0, 1):
                    final = last and par == 1
                    first = 4 * m + 2 * par
                    if not final:
                        sp.wait_ge(y_stored[1 - par], PAIR_STORED * (m + par) + CREDIT)
                        sp.sem_inc(sp_passed, 1)
                        load(first + 2, 1 - par)
                    for j in range(STEPS):
                        k = 8 * m + 4 * par + j
                        for t in (A, B, R):
                            sp.wait_ge(finished, 3 * k + t + 1 + 2)
                            sp.sem_inc(sp_passed, 1)
                            store(first, par, t, j)
                        if not (final and j >= 2):
                            sp.wait_ge(low_ready[R], k + 3)
                            sp.wait_ge(products, 12 * k + 12)
                            stack(k + 2, j % 2)

            with sp.Fori(0, PAIRS // 2 - 1) as m:
                body(m)
            body(PAIRS // 2 - 1, last=True)
            for par in (0, 1):
                sp.wait_ge(y_stored[par], PAIR_STORED * PAIRS // 2 + CREDIT)

        @block.tensor
        def _(pe):
            def average(round_no, bank):
                src = [(moments[:, t, 0:1] if round_no == 0 else spread[:, t:t + 1]) for t in range(3)]
                terms = [(A, [(AA, A), (RA0, R)]), (B, [(AA, B), (RA1, R)]), (R, [(AR0, A), (AR1, B), (RR, R)])]
                for t, parts in terms:
                    for i, (mat, s) in enumerate(parts):
                        mm = nc.tensor.matmul(ps[:, bank, STAT + t:STAT + t + 1], mats[:, mat], src[s],
                                              start=(i == 0), stop=(i == len(parts) - 1))
                mm.then_inc(moments_out, 1)

            def conv(g_par, t, kp, before=None):
                for s in ORDER:
                    if before and s == ORDER[3]:
                        before()
                    bank = 4 * g_par + s
                    images = (t,) if t != R else (0, 1)
                    couts = slice(0, P) if t != R else slice(P, CH)
                    terms = []
                    for kx in range(KX):
                        terms += [(ua[:, 0, s, kx, couts], lambda i, kx=kx: va[:, kp, i, 0, s, :, kx:kx + W]),
                                  (ua[:, 1, s, kx, couts], lambda i, kx=kx: va[:, kp, i, 0, s, :, kx:kx + W]),
                                  (ua[:, 0, s, kx, couts], lambda i, kx=kx: va[:, kp, i, 1, s, :, kx:kx + W])]
                    for kx in range(KX):
                        terms.append((ur[:, s, kx, couts], lambda i, kx=kx: st[:, kp, i, 0, s, :, kx:kx + W]))
                    terms.append((ul[:, s, KX - 1, couts], lambda i: st[:, kp, i, 0, s, :, KX - 1:KX - 1 + W]))
                    terms.append((us[:, s, couts], lambda i: st[:, kp, i, 1, s, :, 0:W]))
                    for n, (lhs, rhs) in enumerate(terms):
                        for i in images:
                            at = slice(0, P) if t != R else slice(i * REST, (i + 1) * REST)
                            mm = nc.tensor.matmul(ps[at, bank, 0:N], lhs, rhs(i),
                                                  start=(n == 0), stop=(n == len(terms) - 1))
                    mm.then_inc(products, 1)

            pe.wait_ge(const_loaded, 80)
            pe.wait_ge(cleared, 1)
            pe.wait_ge(diag_ready, 1)
            nc.tensor.matmul(ps[:, 0, 0:P], ones[:], diag[:, 0], start=True, stop=True)
            nc.tensor.matmul(ps[:, 1, 0:REST], ones[0:REST], diag[0:REST, 1, 0:REST], start=True, stop=True)\
              .then_inc(spread_out, 1)
            for rnd in (0, 1):
                pe.wait_ge(moments_in, rnd + 1)
                average(rnd, 4 + rnd)
            pe.wait_ge(weights_ready, 1)
            pe.wait_ge(moments_read, 2)

            def body(n, last=False):
                for j in range(STEPS):
                    k = 4 * n + j
                    kp = j % 2
                    for t in (A, B, R):
                        g_par = (j + t) % 2
                        pe.wait_ge(finished, 3 * k + t + 1)
                        rnd = {(1, R): 0, (2, A): 1}.get((j, t))
                        before = None
                        if rnd is not None and not last:
                            pe.wait_ge(moments_in, 2 * n + 3 + rnd)
                            average(rnd, 4 * g_par + ORDER[3])
                            before = lambda rnd=rnd: pe.wait_ge(moments_read, 2 * n + 3 + rnd)
                        if t != R:
                            pe.wait_ge(low_ready[t], k + 1)
                        if t == A:
                            pe.wait_ge(stacked[kp], STACK_INC * (2 * n + j // 2 + 1))
                        conv(g_par, t, kp, before)

            with pe.Fori(0, PAIRS - 1) as n:
                body(n)
            body(PAIRS - 1, last=True)

        @block.scalar
        def _(act):
            def high(q, q_par, t, kp):
                act.wait_ge(v_ready, q + 1)
                to = va[:, kp, t, 0] if t != R else vr[:, 0]
                nc.scalar.copy(to[:, :, :, 1:1 + W].rearrange("p s t c -> p (s t) c"),
                               v[:, q_par].rearrange("p s t c -> p (s t) c")).then_inc(high_ready, 1)

            def deviation(p):
                act.wait_ge(var_ready, p + 1)
                nc.scalar.activation(sd[:], ve[:], ACT.Sqrt).then_inc(sd_ready, 1)

            act.wait_ge(cleared, 3)
            act.wait_ge(const_loaded, 80)
            deviation(0)
            for q, (t, k) in enumerate(PROLOGUE):
                if k == 1:
                    act.wait_ge(stacked[0], STACK_INC)
                high(q, q % 2, t, k % 2)

            act.wait_ge(weights_ready, 1)

            def body(m, last=False):
                for par in (0, 1):
                    final = last and par == 1
                    for j in range(STEPS):
                        k = 8 * m + 4 * par + j
                        for t in (A, B, R):
                            g_par = (j + t) % 2
                            act.wait_ge(products, 12 * k + 4 * t + 1)
                            nc.scalar.activation(m1[:, g_par], ps[:, 4 * g_par + SLOT[1], 0:N], ACT.Identity,
                                                 bias=biases[:, t // 2:t // 2 + 1],
                                                 scale=unscale[:, t // 2:t // 2 + 1]).then_inc(m1_ready, 1)
                            if final and j + 1 + t // 2 >= STEPS:
                                continue
                            if t == R:
                                act.wait_ge(stacked[(j + 1) % 2], STACK_INC * (4 * m + 2 * par + (j + 1) // 2 + 1))
                            high(LEAD + 3 * k + t, (LEAD + j + t) % 2, t, (j + 1) % 2)
                            if (j, t) == (1, R) and not final:
                                deviation(2 * m + par + 1)

            with act.Fori(0, PAIRS // 2 - 1) as m:
                body(m)
            body(PAIRS // 2 - 1, last=True)

        @block.vector
        def _(dve):
            setup_steps = [0]

            def link(ins):
                setup_steps[0] += 1
                ins.then_inc(set_dve, 1)
                dve.wait_ge(set_dve, setup_steps[0])

            def unit_stats(t, par, m):
                dve.wait_ge(x_loaded[par][t], UNIT_INC[t] * (m + 1))
                xs = xt[:, par, t].rearrange("p h w -> p (h w)")
                for c in range(CHUNKS):
                    nc.vector.bn_stats(bn[:, t, c], xs[:, c * CHUNK:(c + 1) * CHUNK]).then_inc(stat_dve, 1)

            CHAIN = 3 * CHUNKS + 3 + 9

            def aggregate(p):
                dve.wait_ge(stat_dve, CHAIN * p + 3 * CHUNKS)
                dve.sem_inc(dve_passed, 1)
                for t in range(3):
                    ins = nc.vector.bn_aggr(moments[:, t], bn[:, t].rearrange("p c s -> p (c s)"))
                    ins.then_inc(stat_dve, 1)
                dve.wait_ge(stat_dve, CHAIN * p + 3 * CHUNKS + 3)
                dve.sem_inc(moments_in, 1)

            def link_stat(ins, p, i):
                ins.then_inc(stat_dve, 1)
                dve.wait_ge(stat_dve, CHAIN * p + 3 * CHUNKS + 3 + i)

            def group_mean(p, par, bank):
                dve.wait_ge(moments_out, 2 * p + 1)
                link_stat(nc.vector.tensor_copy(mean[:, par], ps[:, bank, STAT:STAT + 3]), p, 1)
                dve.sem_inc(moments_read, 1)
                link_stat(nc.vector.tensor_tensor(dev[:], moments[:, :, 0], mean[:, par], ALU.subtract), p, 2)
                link_stat(nc.vector.tensor_tensor(dev[:], dev[:], dev[:], ALU.mult), p, 3)
                link_stat(nc.vector.tensor_tensor(spread[:], dev[:], moments[:, :, 1], ALU.add), p, 4)
                dve.sem_inc(moments_in, 1)

            def group_var(p, bank):
                dve.wait_ge(moments_out, 2 * p + 2)
                link_stat(nc.vector.tensor_scalar(ve[:], ps[:, bank, STAT:STAT + 3], EPS, None, ALU.add), p, 5)
                dve.sem_inc(moments_read, 1)
                dve.sem_inc(var_ready, 1)

            def group_rstd(p, par):
                dve.wait_ge(sd_ready, p + 1)
                link_stat(nc.vector.reciprocal(r0[:], sd[:]), p, 6)
                link_stat(nc.vector.tensor_tensor(r1[:], ve[:], r0[:], ALU.mult), p, 7)
                link_stat(nc.vector.scalar_tensor_tensor(r1[:], r1[:], -0.5, r0[:], ALU.mult, ALU.mult), p, 8)
                nc.vector.tensor_scalar(r1[:], r1[:], V_SCALE, 1.5 * V_SCALE, ALU.mult, ALU.add)\
                  .then_inc(stat_dve, 1)
                dve.wait_ge(stat_dve, CHAIN * p + 3 * CHUNKS + 3 + 9)
                nc.vector.tensor_tensor(rstd[:, par], r0[:], r1[:], ALU.mult).then_inc(rstd_ready, 1)
                dve.wait_ge(rstd_ready, p + 1)

            def normalise(q_par, t, par, j):
                g = norm[:, q_par]
                top, bottom = max(j * ROWS - 1, 0), min((j + 1) * ROWS + 1, H)
                at = top - (j * ROWS - 1)
                if j == 0:
                    nc.vector.memset(g[:, 0], 0.0)
                if j == STEPS - 1:
                    nc.vector.memset(g[:, ROWS + 1], 0.0)
                nc.vector.tensor_scalar(g[:, at:at + bottom - top], xt[:, par, t, top:bottom],
                                        mean[:, par, t:t + 1], rstd[:, par, t:t + 1],
                                        ALU.subtract, ALU.mult).then_inc(normed, 1)

            def transform(q, q_par):
                dve.wait_ge(normed, q + 1)
                to = v[:, q_par]
                g = norm[:, q_par].rearrange("p (t two) c -> p two t c", two=2)
                d1, d2 = g[:, 1, 0:TILES], g[:, 0, 1:TILES + 1]
                nc.vector.tensor_tensor(to[:, 0:2], g[:, :, 0:TILES], g[:, :, 1:TILES + 1], ALU.subtract)
                nc.vector.tensor_tensor(to[:, SLOT[1]], d1, d2, ALU.add)
                nc.vector.tensor_tensor(to[:, SLOT[2]], d2, d1, ALU.subtract).then_inc(v_ready, 1)

            def low(q, q_par, t, kp):
                dve.wait_ge(high_ready, q + 1)
                src = va[:, kp, t] if t != R else vr
                view = lambda part: src[:, part, :, :, 1:1 + W].rearrange("p s t c -> p (s t) c")
                nc.vector.tensor_tensor(view(1), v[:, q_par].rearrange("p s t c -> p (s t) c"), view(0),
                                        ALU.subtract).then_inc(low_ready[t], 1)

            rows = lambda ap: ap.rearrange("p (t c) -> p t c", c=W)

            def form_halves(k, t, g_par):
                dve.wait_ge(m1_ready, 3 * k + t + 1)
                dve.wait_ge(products, 12 * k + 4 * t + 2)
                m2 = ps[:, 4 * g_par + SLOT[2], 0:N]
                c = t // 2
                nc.vector.scalar_tensor_tensor(even[:, g_par], m2, unscale[:, c:c + 1], m1[:, g_par],
                                               ALU.mult, ALU.add)
                nc.vector.scalar_tensor_tensor(odd[:, g_par], m2, minus[:, c:c + 1], m1[:, g_par],
                                               ALU.mult, ALU.add).then_inc(halves, 1)

            def add_x(k, t, g_par, par, j):
                dve.wait_ge(halves, 3 * k + t + 1)
                y = xt[:, par, t, j * ROWS:(j + 1) * ROWS].rearrange("p (t two) c -> p two t c", two=2)
                nc.vector.tensor_tensor(rows(even[:, g_par]), rows(even[:, g_par]), y[:, 0], ALU.add)
                nc.vector.tensor_tensor(rows(odd[:, g_par]), rows(odd[:, g_par]), y[:, 1], ALU.add)\
                  .then_inc(residual, 1)

            def finish(k, t, g_par, par, j):
                dve.wait_ge(residual, 3 * k + t + 1)
                dve.wait_ge(products, 12 * k + 4 * t + 4)
                y = xt[:, par, t, j * ROWS:(j + 1) * ROWS].rearrange("p (t two) c -> p two t c", two=2)
                c = t // 2
                nc.vector.scalar_tensor_tensor(y[:, 0], rows(ps[:, 4 * g_par + SLOT[0], 0:N]), unscale[:, c:c + 1],
                                               rows(even[:, g_par]), ALU.mult, ALU.add)
                nc.vector.scalar_tensor_tensor(y[:, 1], rows(ps[:, 4 * g_par + SLOT[3], 0:N]), minus[:, c:c + 1],
                                               rows(odd[:, g_par]), ALU.mult, ALU.add).then_inc(finished, 1)

            nc.vector.memset(ones[:], 1.0).then_inc(cleared, 1)
            for tile_ in (va[:].rearrange("p a b c s t w -> p (a b c s t) w"),
                          vr[:].rearrange("p c s t w -> p (c s t) w")):
                nc.vector.memset(tile_[:, :, 0:WP:WP - 1], 0.0).then_inc(cleared, 1)
            dve.sem_inc(finished, 2)

            dve.wait_ge(w_loaded, 96)
            for c in (0, 1):
                nc.vector.tensor_reduce(scales[:, 0, c:c + 1], wr[c], AX.X, ALU.max).then_inc(set_dve, 1)
                nc.vector.tensor_reduce(scales[:, 1, c:c + 1], wr[c], AX.X, ALU.min).then_inc(set_dve, 1)
            setup_steps[0] = 4
            dve.wait_ge(set_dve, 4)
            link(nc.vector.scalar_tensor_tensor(scales[:, 2], scales[:, 1], -1.0, scales[:, 0],
                                                ALU.mult, ALU.max))
            link(nc.vector.tensor_scalar(scales[:, 3], scales[:, 2], LEAST, None, ALU.max))
            link(nc.vector.tensor_scalar(scales[:, 4].bitcast(I32), scales[:, 3].bitcast(I32), EXPONENT, None,
                                         ALU.bitwise_and))
            link(nc.vector.tensor_scalar(unscale[:], scales[:, 4], 1.0 / (U_SCALE * V_SCALE), None, ALU.mult))
            link(nc.vector.tensor_scalar(minus[:], unscale[:], -1.0, None, ALU.mult))
            link(nc.vector.reciprocal(scales[:, 5], unscale[:]))
            dve.wait_ge(const_loaded, 80)
            for c in (0, 1):
                link(nc.vector.tensor_scalar(diag[:, c], ident[:], scales[:, 5, c:c + 1], 1.0 / V_SCALE,
                                             ALU.mult, ALU.mult))
            dve.sem_inc(diag_ready, 1)

            for t in (A, B, R):
                unit_stats(t, 0, 0)
            aggregate(0)

            dve.wait_ge(spread_out, 1)
            link(nc.vector.tensor_copy(row_scale[:, 0:P], ps[:, 0, 0:P]))
            link(nc.vector.tensor_copy(row_scale[:, P:CH], ps[:, 1, 0:REST]))
            group_mean(0, 0, 4)
            for c in (0, 1):
                for i in range(3):
                    for kx in range(KX):
                        ins = nc.vector.tensor_tensor(wc[c][:, i, kx], wc[c][:, i, kx], row_scale[:], ALU.mult)
                link(ins)
                if c == 0:
                    group_var(0, 5)
                g0, g1, g2 = (wc[c][:, i] for i in range(3))
                link(nc.vector.tensor_copy(u[:, SLOT[0]], g0))
                link(nc.vector.tensor_copy(u[:, SLOT[3]], g2))
                link(nc.vector.tensor_tensor(g0, g0, g2, ALU.add))
                link(nc.vector.tensor_tensor(u[:, SLOT[1]], g0, g1, ALU.add))
                link(nc.vector.tensor_tensor(u[:, SLOT[2]], g0, g1, ALU.subtract))
                half = u[:, 2:4]
                link(nc.vector.tensor_scalar(half, half, 0.5, None, ALU.mult))
                high_, low_ = (ua[:, 0], ua[:, 1]) if c == 0 else (ur[:], ul[:])
                link(nc.vector.tensor_copy(high_, u))
                link(nc.vector.tensor_tensor(low_, u, high_, ALU.subtract))
                if c == 0:
                    group_rstd(0, 0)
            for i in (0, 1):
                mine = slice(i * REST, (i + 1) * REST)
                link(nc.vector.tensor_copy(us[mine], ul[mine, :, i]))
            dve.sem_inc(weights_ready, 1)

            normalise(0, R, 0, 0)
            following = PROLOGUE[1:] + [(A, 1)]
            for q, (t, k) in enumerate(PROLOGUE):
                transform(q, q % 2)
                nt, nk = following[q]
                normalise((q + 1) % 2, nt, 0, nk)
                low(q, q % 2, t, k % 2)

            def body(m, last=False):
                for par in (0, 1):
                    final = last and par == 1
                    for j in range(STEPS):
                        k = 8 * m + 4 * par + j
                        for t in (A, B, R):
                            g_par = (j + t) % 2
                            q, q_par = LEAD + 3 * k + t, (LEAD + j + t) % 2
                            prepares = not (final and j + 1 + t // 2 >= STEPS)
                            if prepares:
                                transform(q, q_par)
                            form_halves(k, t, g_par)
                            nt = (t + 1) % 3
                            nj = j + {A: 1, B: 2, R: 2}[t]
                            if not (final and nj >= STEPS):
                                normalise(1 - q_par, nt, (par + nj // STEPS) % 2, nj % STEPS)
                            add_x(k, t, g_par, par, j)
                            if prepares:
                                low(q, q_par, t, (j + 1) % 2)
                            finish(k, t, g_par, par, j)
                            if final:
                                continue
                            p, p_par = 2 * m + par + 1, 1 - par
                            if (j, t) in ((0, B), (0, R), (1, A)):
                                unit_stats({(0, B): A, (0, R): B, (1, A): R}[j, t], p_par, m + par)
                            if (j, t) == (1, A):
                                aggregate(p)
                            if (j, t) == (1, B):
                                group_mean(p, p_par, 4 * ((1 + R) % 2) + ORDER[3])
                            if (j, t) == (1, R):
                                group_var(p, 4 * (2 % 2) + ORDER[3])
                            if (j, t) == (2, A):
                                group_rstd(p, p_par)

            with dve.Fori(0, PAIRS // 2 - 1) as m:
                body(m)
            body(PAIRS // 2 - 1, last=True)


def kernel(x, L0_conv_weight, L0_conv_bias):
    import concourse.bacc as bacc
    from concourse.bass_utils import run_bass_kernel_spmd

    weight = np.ascontiguousarray(L0_conv_weight)
    arrays = {
        "x": np.ascontiguousarray(x),
        "w_rows": weight,
        "w_cols": np.ascontiguousarray(weight.reshape(CH, CH, 3, KX).transpose(1, 2, 3, 0)),
        "bias": np.ascontiguousarray(L0_conv_bias).reshape(CH, 1),
        "matrices": group_matrices(),
        "identity": np.eye(P, dtype=np.float32),
    }
    nc = bacc.Bacc("TRN2", target_bir_lowering=False, num_devices=1)
    args = [nc.dram_tensor(name, a.shape, F32, kind="ExternalInput").ap() for name, a in arrays.items()]
    out = nc.dram_tensor("out", (IMAGES, CH, H, W), F32, kind="ExternalOutput").ap()
    preact_conv(nc, *args, out)
    r = run_bass_kernel_spmd(nc, [arrays], core_ids=[0])
    return r.results[0]["out"]
```

```python
from contextlib import ExitStack

import numpy as np

import concourse.bass as bass
from concourse import mybir

F32 = mybir.dt.float32
F16 = mybir.dt.float16
BF16 = mybir.dt.bfloat16
I32 = mybir.dt.int32
ALU = mybir.AluOpType
ACT = mybir.ActivationFunctionType
AX = mybir.AxisListType

P = 128
IMAGES, CH, H, W = 32, 192, 56, 56
REST = CH - P
GROUPS, EPS = 32, 1e-5
PER_GROUP = CH // GROUPS
KX = 3
TAPS = 3 * KX
PAIRS = IMAGES // 2

OUT = 4
POINTS = OUT + 2
TILES = (4, 4, 4, 2)
STEPS = len(TILES)
FIRST_ROW = [OUT * sum(TILES[:j]) for j in range(STEPS)]
MAXT = max(TILES)
WP = W + 2
assert OUT * sum(TILES) == H

SLOT = {1: 0, 3: 1, 2: 2, 4: 3, 0: 4, 5: 5}
BANKS = POINTS // 2

A, B, R = 0, 1, 2
V_SCALE = 32.0
U_SCALE = 2.0 ** 14
LEAST = 2.0 ** -100
EXPONENT = 0x7F800000

PROLOGUE = [(R, 0), (A, 0), (B, 0), (R, 1)]
LEAD = len(PROLOGUE)


def group_matrices():
    a = np.arange(P) // PER_GROUP
    r = (P + np.arange(P) % REST) // PER_GROUP
    image = np.arange(P) // REST
    aa = a[:, None] == a[None]
    ra = r[:, None] == a[None]
    ar = a[:, None] == r[None]
    rr = (r[:, None] == r[None]) & (image[:, None] == image[None])
    mats = [aa, ra & (image[:, None] == 0), ra & (image[:, None] == 1),
            ar & (image[None] == 0), ar & (image[None] == 1), rr]
    return (np.stack(mats, axis=1) / PER_GROUP).astype(np.float32)


AA, RA0, RA1, AR0, AR1, RR = range(6)


def preact_conv(nc, x, w_rows, w_cols, bias, matrices, identity, out):
    with ExitStack() as ctx:
        def sb(name, shape, dt=F32):
            return ctx.enter_context(nc.sbuf_tensor(name, shape, dt))

        def sem(name):
            return ctx.enter_context(nc.semaphore(name))

        xt = sb("xt", [P, 2, 3, H, W])
        norm = sb("norm", [P, 2, OUT * MAXT + 2, W])
        diff = sb("diff", [P, MAXT, OUT, W])
        quad = sb("quad", [P, MAXT, 2, W])
        v = sb("v", [P, MAXT, POINTS, W])
        va = sb("va", [P, 2, 2, 2, MAXT, POINTS, WP], F16)
        vr = sb("vr", [P, 2, MAXT, POINTS, WP], F16)
        st = sb("st", [P, 2, 2, 2, MAXT, POINTS, WP], F16)
        m13 = sb("m13", [P, 2, 2 * MAXT * W])
        sums = sb("sums", [P, 2, 2 * MAXT * W])
        difs = sb("difs", [P, 2, 2 * MAXT * W])
        part = sb("part", [P, MAXT, OUT, W])

        ua = sb("ua", [P, 2, POINTS, KX, CH], F16)
        ur = sb("ur", [P, POINTS, KX, CH], F16)
        ul = sb("ul", [P, POINTS, CH], F16)
        us = sb("us", [P, POINTS, CH], F16)

        mats = sb("mats", [P, 6, P])
        ident = sb("ident", [P, P])
        ones = sb("ones", [P, P])
        biases = sb("biases", [P, 2])
        unscale = sb("unscale", [P, 2])
        minus = sb("minus", [P, 2])
        scales = sb("scales", [P, 6, 2])
        diag = sb("diag", [P, 2, P])
        row_scale = sb("row_scale", [P, CH])

        unread = sb("unread", [P, H * W], BF16)
        total = sb("total", [P, 3])
        neg_mean = sb("neg_mean", [P, 3])
        squares = sb("squares", [P, 3])
        ch_mean = sb("ch_mean", [P, 3])
        ch_var = sb("ch_var", [P, 3])
        mean = sb("mean", [P, 3])
        dev = sb("dev", [P, 3])
        spread = sb("spread", [P, 3])
        ve = sb("ve", [P, 3])
        sd = sb("sd", [P, 3])
        r0 = sb("r0", [P, 3])
        r1 = sb("r1", [P, 3])
        rstd = sb("rstd", [P, 2, 3])
        shift = sb("shift", [P, 2, 3])

        flat = xt[:, 1, :, :, :].rearrange("p u h w -> p (u h w)")
        WIDE = TAPS * CH
        wr = [flat[:, i * WIDE:(i + 1) * WIDE] for i in (0, 1)]
        wc = [flat[:, i * WIDE:(i + 1) * WIDE].rearrange("p (i k o) -> p i k o", i=3, k=KX)
              for i in (2, 3)]
        PLANE = KX * CH
        u = [flat[:, at:at + 4 * PLANE].rearrange("p (s n) -> p s n", s=4) for at in (0, 4 * WIDE)]
        low_rest = st[:, 1].rearrange("p i a t s c -> p (i a t s c)")[:, 0:POINTS * PLANE]\
            .rearrange("p (s k o) -> p s k o", s=POINTS, k=KX)

        ps = ctx.enter_context(nc.psum_tensor("ps", [P, 8, 512], F32))
        STAT = 2 * BANKS

        x_loaded = [[sem(f"x_loaded{p}{t}") for t in range(3)] for p in range(2)]
        rows_loaded = sem("rows_loaded")
        cols_loaded = [sem("cols_loaded0"), sem("cols_loaded1")]
        ident_loaded = sem("ident_loaded")
        const_loaded = sem("const_loaded")
        cleared = sem("cleared")
        set_dve = sem("set_dve")
        diag_ready = sem("diag_ready")
        spread_out = sem("spread_out")
        planes_ready = sem("planes_ready")
        weights_high = sem("weights_high")
        weights_ready = sem("weights_ready")
        summed = sem("summed")
        moments_in = sem("moments_in")
        moments_out = sem("moments_out")
        var_ready = sem("var_ready")
        sd_ready = sem("sd_ready")
        stat_dve = sem("stat_dve")
        rstd_ready = sem("rstd_ready")
        sp_passed = sem("sp_passed")
        edged = sem("edged")
        normed = sem("normed")
        diffed = sem("diffed")
        v_ready = sem("v_ready")
        high_ready = sem("high_ready")
        low_ready = [sem(f"low_ready{t}") for t in range(3)]
        stacked = [sem("stacked0"), sem("stacked1")]
        products = sem("products")
        m13_ready = sem("m13_ready")
        halves = sem("halves")
        combined = sem("combined")
        residual = sem("residual")
        finished = sem("finished")
        y_stored = [sem("y_stored0"), sem("y_stored1")]

        STACK_INC = 8 * 16
        UNIT_INC = [16, 16, 32]
        PAIR_STORED = STEPS * sum(UNIT_INC)
        SUMS, EXTRA = 7, 2
        UPARTS = 4
        FREE = 2
        CREDIT = 16

        def outside(j):
            return (j == 0) + (j == STEPS - 1)

        def edges_before(j, t):
            order = [(R, 0), (A, 0), (B, 0), (R, 1), (A, 1), (B, 1), (R, 2), (A, 2), (B, 2), (R, 3), (A, 3), (B, 3)]
            return sum(outside(jj) for _, jj in order[:order.index((t, j)) + 1])

        def u_parts(c):
            high_, low_ = (ua[:, 0], ua[:, 1]) if c == 0 else (ur[:], low_rest)
            g0, g2 = (wc[c][:, i].rearrange("p k o -> p (k o)") for i in (0, 2))
            for slots, planes, f in ((slice(0, 4, 2), u[c][:, 0:4:2], -1.0 / 6),
                                     (slice(1, 4, 2), u[c][:, 1:4:2], 1.0 / 24),
                                     (SLOT[0], g0, 0.25), (SLOT[5], g2, 1.0)):
                to = "p s k o -> p s (k o)" if isinstance(slots, slice) else "p k o -> p (k o)"
                yield high_[:, slots].rearrange(to), low_[:, slots].rearrange(to), planes, f

        block = ctx.enter_context(nc.Block())

        @block.sync
        def _(sp):
            def load(first, par, units=(A, B, R)):
                for t in units:
                    if t != R:
                        sp.dma_start(xt[:, par, t],
                                     x[bass.ds(first + t, 1), 0:P].rearrange("n c h w -> (n c) h w"))\
                          .then_inc(x_loaded[par][t], 16)
                for i in (0, 1) if R in units else ():
                    sp.dma_start(xt[i * REST:(i + 1) * REST, par, R],
                                 x[bass.ds(first + i, 1), P:CH].rearrange("n c h w -> (n c) h w"))\
                      .then_inc(x_loaded[par][R], 16)

            def store(first, par, t, j):
                rows = slice(FIRST_ROW[j], FIRST_ROW[j] + OUT * TILES[j])
                if t != R:
                    sp.dma_start(out[bass.ds(first + t, 1), 0:P, rows].rearrange("n c h w -> (n c) h w"),
                                 xt[:, par, t, rows]).then_inc(y_stored[par], 16)
                else:
                    for i in (0, 1):
                        sp.dma_start(out[bass.ds(first + i, 1), P:CH, rows].rearrange("n c h w -> (n c) h w"),
                                     xt[i * REST:(i + 1) * REST, par, t, rows]).then_inc(y_stored[par], 16)

            def stack(j, sp_):
                n = TILES[j] * POINTS * WP
                for i in (0, 1):
                    mine = slice(i * REST, (i + 1) * REST)
                    high = vr[mine, 0].rearrange("p t s c -> p (t s c)")
                    low = vr[mine, 1].rearrange("p t s c -> p (t s c)")
                    s1 = st[:, sp_, i, 0].rearrange("p t s c -> p (t s c)")
                    s2 = st[:, sp_, i, 1].rearrange("p t s c -> p (t s c)")
                    sp.dma_start(s1[0:REST, 0:n], high[:, 0:n]).then_inc(stacked[sp_], 16)
                    sp.dma_start(s1[REST:P, 0:n], low[:, 0:n]).then_inc(stacked[sp_], 16)
                    sp.dma_start(s2[0:REST, 0:n], high[:, 0:n]).then_inc(stacked[sp_], 16)
                    sp.dma_start(s2[REST:P, 0:n - 1], high[:, 1:n]).then_inc(stacked[sp_], 16)

            sp.dma_start(wr[0], w_rows[0:P]).then_inc(rows_loaded, 16)
            for i in (0, 1):
                sp.dma_start(wr[1][i * REST:(i + 1) * REST], w_rows[P:CH]).then_inc(rows_loaded, 16)
            sp.dma_start(ident[:], identity).then_inc(ident_loaded, 16)
            load(0, 0, (A,))
            sp.dma_start(wc[0], w_cols[0:P]).then_inc(cols_loaded[0], 16)
            load(0, 0, (B, R))
            for i in (0, 1):
                sp.dma_start(wc[1][i * REST:(i + 1) * REST], w_cols[P:CH]).then_inc(cols_loaded[1], 16)
            sp.dma_start(mats[:], matrices).then_inc(const_loaded, 16)
            sp.dma_start(biases[:, 0:1], bias[0:P]).then_inc(const_loaded, 16)
            for i in (0, 1):
                sp.dma_start(biases[i * REST:(i + 1) * REST, 1:2], bias[P:CH]).then_inc(const_loaded, 16)
            for par in (0, 1):
                sp.sem_inc(y_stored[par], CREDIT)
            for k in (0, 1):
                sp.wait_ge(low_ready[R], k + 1)
                stack(k, k % 2)
            sp.wait_ge(weights_ready, 1)

            def body(m, last=False):
                for par in (0, 1):
                    final = last and par == 1
                    first = 4 * m + 2 * par
                    if not final:
                        sp.wait_ge(y_stored[1 - par], PAIR_STORED * (m + par) + CREDIT)
                        sp.sem_inc(sp_passed, 1)
                        load(first + 2, 1 - par)
                    for j in range(STEPS):
                        k = 8 * m + 4 * par + j
                        for t in (A, B, R):
                            sp.wait_ge(finished, 3 * k + t + 1 + FREE)
                            sp.sem_inc(sp_passed, 1)
                            store(first, par, t, j)
                        if not (final and j >= 2):
                            sp.wait_ge(low_ready[R], k + 3)
                            sp.sem_inc(sp_passed, 1)
                            sp.wait_ge(products, 3 * BANKS * (k + 1))
                            stack((j + 2) % STEPS, j % 2)

            with sp.Fori(0, PAIRS // 2 - 1) as m:
                body(m)
            body(PAIRS // 2 - 1, last=True)
            for par in (0, 1):
                sp.wait_ge(y_stored[par], PAIR_STORED * PAIRS // 2 + CREDIT)

        @block.tensor
        def _(pe):
            def average(rnd):
                src = (ch_mean, spread)[rnd]
                terms = [(A, [(AA, A), (RA0, R)]), (B, [(AA, B), (RA1, R)]), (R, [(AR0, A), (AR1, B), (RR, R)])]
                for t, parts in terms:
                    for i, (mat, s) in enumerate(parts):
                        mm = nc.tensor.matmul(ps[:, STAT + rnd, t:t + 1], mats[:, mat], src[:, s:s + 1],
                                              start=(i == 0), stop=(i == len(parts) - 1))
                mm.then_inc(moments_out, 1)

            def bank_of_products(b, g_par, t, j):
                n, kp = TILES[j], j % 2
                images = (t,) if t != R else (0, 1)
                couts = slice(0, P) if t != R else slice(P, CH)
                for s in (2 * b, 2 * b + 1):
                    at_cols = slice((s % 2) * n * W, (s % 2 + 1) * n * W)

                    def parts(i, part, kx):
                        return va[:, kp, i, part, 0:n, s, kx:kx + W]

                    def stacks(i, which, kx):
                        return st[:, kp, i, which, 0:n, s, kx:kx + W]

                    terms = []
                    for kx in range(KX):
                        terms += [(ua[:, 0, s, kx, couts], parts, 0, kx),
                                  (ua[:, 1, s, kx, couts], parts, 0, kx),
                                  (ua[:, 0, s, kx, couts], parts, 1, kx)]
                    terms += [(ur[:, s, kx, couts], stacks, 0, kx) for kx in range(KX)]
                    terms += [(ul[:, s, couts], stacks, 0, KX - 1), (us[:, s, couts], stacks, 1, 0)]
                    for i_term, (lhs, tile_of, which, kx) in enumerate(terms):
                        for i in images:
                            at = slice(0, P) if t != R else slice(i * REST, (i + 1) * REST)
                            mm = nc.tensor.matmul(ps[at, BANKS * g_par + b, at_cols], lhs, tile_of(i, which, kx),
                                                  start=(i_term == 0), stop=(i_term == len(terms) - 1))
                mm.then_inc(products, 1)

            pe.wait_ge(cleared, 1)
            pe.wait_ge(diag_ready, 1)
            nc.tensor.matmul(ps[:, 0, 0:P], ones[:], diag[:, 0], start=True, stop=True)
            nc.tensor.matmul(ps[:, 1, 0:REST], ones[0:REST], diag[0:REST, 1, 0:REST], start=True, stop=True)\
              .then_inc(spread_out, 1)
            pe.wait_ge(const_loaded, 64)
            for rnd in (0, 1):
                pe.wait_ge(moments_in, rnd + 1)
                average(rnd)
            pe.wait_ge(weights_ready, 1)

            def body(n, last=False):
                for j in range(STEPS):
                    k = STEPS * n + j
                    for t in (A, B, R):
                        g_par = (j + t) % 2
                        if t != R:
                            pe.wait_ge(low_ready[t], k + 1)
                        if t == A:
                            pe.wait_ge(stacked[j % 2], STACK_INC * (2 * n + j // 2 + 1))
                        for b in range(BANKS):
                            rnd = {(2, B, 1): 0, (2, R, 0): 1}.get((j, t, b))
                            if rnd is not None and not last:
                                pe.wait_ge(moments_in, 2 * n + 3 + rnd)
                                average(rnd)
                            pe.wait_ge((m13_ready, halves, finished)[b], 3 * k + t + 1)
                            bank_of_products(b, g_par, t, j)

            with pe.Fori(0, PAIRS - 1) as n:
                body(n)
            body(PAIRS - 1, last=True)

        @block.scalar
        def _(act):

            def x_flat(par, t):
                return xt[:, par, t].rearrange("p h w -> p (h w)")

            def sum_x(p, par, t, m):
                act.wait_ge(x_loaded[par][t], UNIT_INC[t] * (m + 1))
                act.wait_ge(summed, SUMS * p + EXTRA + t)
                nc.scalar.activation(unread[:], x_flat(par, t), ACT.Copy, accum_out=total[:, t:t + 1])\
                  .then_inc(summed, 1)

            def negate_means(p):
                act.wait_ge(summed, SUMS * p + EXTRA + 3)
                nc.scalar.mul(neg_mean[:], total[:], -1.0 / (H * W)).then_inc(summed, 1)

            def sum_squares(p, par, t):
                act.wait_ge(summed, SUMS * p + EXTRA + 4 + t)
                nc.scalar.activation(unread[:], x_flat(par, t), ACT.Square, bias=neg_mean[:, t:t + 1],
                                     accum_out=squares[:, t:t + 1]).then_inc(summed, 1)

            def deviation(p):
                act.wait_ge(var_ready, p + 1)
                nc.scalar.activation(sd[:], ve[:], ACT.Sqrt).then_inc(sd_ready, 1)

            def normalise(q_par, t, par, j):
                first, n = FIRST_ROW[j] - 1, OUT * TILES[j] + 2
                top, bottom = max(first, 0), min(first + n, H)
                nc.scalar.activation(norm[:, q_par, top - first:bottom - first], xt[:, par, t, top:bottom],
                                     ACT.Identity, bias=shift[:, par, t:t + 1], scale=rstd[:, par, t:t + 1])\
                  .then_inc(normed, 1)

            def high(q, t, j):
                n = TILES[j]
                act.wait_ge(v_ready, q + 1)
                to = va[:, j % 2, t, 0, 0:n] if t != R else vr[:, 0, 0:n]
                nc.scalar.copy(to[:, :, :, 1:1 + W].rearrange("p t s c -> p (t s) c"),
                               v[:, 0:n].rearrange("p t s c -> p (t s) c")).then_inc(high_ready, 1)

            def first_statistics(t):
                act.wait_ge(x_loaded[0][t], UNIT_INC[t])
                if t != A:
                    act.wait_ge(summed, 3 * t)
                nc.scalar.activation(unread[:], x_flat(0, t), ACT.Copy, accum_out=total[:, t:t + 1])\
                  .then_inc(summed, 1)
                act.wait_ge(summed, 3 * t + 1)
                nc.scalar.mul(neg_mean[:, t:t + 1], total[:, t:t + 1], -1.0 / (H * W)).then_inc(summed, 1)
                act.wait_ge(summed, 3 * t + 2)
                nc.scalar.activation(unread[:], x_flat(0, t), ACT.Square, bias=neg_mean[:, t:t + 1],
                                     accum_out=squares[:, t:t + 1]).then_inc(summed, 1)

            def weights_high_parts(c):
                act.wait_ge(planes_ready, c + 1)
                for high_, _, planes, f in u_parts(c):
                    nc.scalar.mul(high_, planes, f).then_inc(weights_high, 1)

            for t in (A, B, R):
                first_statistics(t)
            for c in (0, 1):
                weights_high_parts(c)
            deviation(0)
            act.wait_ge(cleared, 3)
            act.wait_ge(const_loaded, 64)
            act.wait_ge(rstd_ready, 1)
            normalise(0, R, 0, 0)
            following = PROLOGUE[1:] + [(A, 1)]
            for q, (t, k) in enumerate(PROLOGUE):
                if q:
                    act.wait_ge(v_ready, q)
                nt, nk = following[q]
                normalise((q + 1) % 2, nt, 0, nk)
                if (t, k) == (R, 1):
                    act.wait_ge(stacked[0], STACK_INC)
                high(q, t, k)

            def m1_m3(k, j, t):
                n, g_par, c = TILES[j] * W, (j + t) % 2, t // 2
                act.wait_ge(products, BANKS * (3 * k + t) + 1)
                act.wait_ge(halves, 3 * k + t + 1)
                bank = ps[:, BANKS * g_par]
                nc.scalar.activation(m13[:, g_par, 0:n], bank[:, 0:n], ACT.Identity,
                                     bias=biases[:, c:c + 1], scale=unscale[:, c:c + 1])
                nc.scalar.mul(m13[:, g_par, n:2 * n], bank[:, n:2 * n], unscale[:, c:c + 1])\
                  .then_inc(m13_ready, 1)

            act.wait_ge(weights_ready, 1)
            m1_m3(0, 0, A)

            def body(m, last=False):
                for par in (0, 1):
                    final = last and par == 1
                    p, p_par = 2 * m + par + 1, 1 - par
                    for j in range(STEPS):
                        k = 8 * m + 4 * par + j
                        for t in (A, B, R):
                            if (j, t) == (2, B) and not final:
                                deviation(p)
                            ahead = {A: 1, B: 1, R: 2}[t]
                            if not (final and j + ahead >= STEPS):
                                if t == R:
                                    act.wait_ge(stacked[(j + 1) % 2],
                                                STACK_INC * (4 * m + 2 * par + (j + 1) // 2 + 1))
                                high(LEAD + 3 * k + t, t, (j + ahead) % STEPS)
                            if t != R:
                                m1_m3(k, j, t + 1)
                            elif not (final and j == STEPS - 1):
                                m1_m3(k + 1, (j + 1) % STEPS, A)
                            nt, nj = (t + 1) % 3, j + {A: 1, B: 2, R: 2}[t]
                            if (j, t) == (2, B) and not final:
                                act.wait_ge(rstd_ready, p + 1)
                            if not (final and nj >= STEPS):
                                normalise((LEAD + j + t + 1) % 2, nt, (par + nj // STEPS) % 2, nj % STEPS)
                            if final:
                                continue
                            if (j, t) == (0, B):
                                sum_x(p, p_par, A, m + par)
                            if (j, t) == (0, R):
                                sum_x(p, p_par, B, m + par)
                                sum_x(p, p_par, R, m + par)
                            if (j, t) == (1, A):
                                negate_means(p)
                                sum_squares(p, p_par, A)
                            if (j, t) == (1, B):
                                sum_squares(p, p_par, B)
                                sum_squares(p, p_par, R)

            with act.Fori(0, PAIRS // 2 - 1) as m:
                body(m)
            body(PAIRS // 2 - 1, last=True)

        @block.vector
        def _(dve):
            setup_steps = [0]

            def link(ins):
                setup_steps[0] += 1
                ins.then_inc(set_dve, 1)
                dve.wait_ge(set_dve, setup_steps[0])

            CHAIN = 13

            def link_stat(ins, p, i):
                ins.then_inc(stat_dve, 1)
                dve.wait_ge(stat_dve, CHAIN * p + i)

            def channel_moments(p):
                dve.wait_ge(summed, SUMS * (p + 1) + EXTRA)
                link_stat(nc.vector.tensor_scalar(ch_mean[:], neg_mean[:], -1.0, None, ALU.mult), p, 1)
                link_stat(nc.vector.tensor_scalar(ch_var[:], squares[:], 1.0 / (H * W), None, ALU.mult), p, 2)
                dve.sem_inc(moments_in, 1)

            def group_mean(p):
                dve.wait_ge(moments_out, 2 * p + 1)
                link_stat(nc.vector.tensor_copy(mean[:], ps[:, STAT, 0:3]), p, 3)
                link_stat(nc.vector.tensor_tensor(dev[:], ch_mean[:], mean[:], ALU.subtract), p, 4)
                link_stat(nc.vector.tensor_tensor(dev[:], dev[:], dev[:], ALU.mult), p, 5)
                link_stat(nc.vector.tensor_tensor(spread[:], dev[:], ch_var[:], ALU.add), p, 6)
                dve.sem_inc(moments_in, 1)

            def group_var(p):
                dve.wait_ge(moments_out, 2 * p + 2)
                link_stat(nc.vector.tensor_scalar(ve[:], ps[:, STAT + 1, 0:3], EPS, None, ALU.add), p, 7)
                dve.sem_inc(var_ready, 1)

            def group_rstd(p, par):
                dve.wait_ge(sd_ready, p + 1)
                link_stat(nc.vector.reciprocal(r0[:], sd[:]), p, 8)
                link_stat(nc.vector.tensor_tensor(r1[:], ve[:], r0[:], ALU.mult), p, 9)
                link_stat(nc.vector.scalar_tensor_tensor(r1[:], r1[:], -0.5, r0[:], ALU.mult, ALU.mult), p, 10)
                link_stat(nc.vector.tensor_scalar(r1[:], r1[:], V_SCALE, 1.5 * V_SCALE, ALU.mult, ALU.add), p, 11)
                link_stat(nc.vector.tensor_tensor(rstd[:, par], r0[:], r1[:], ALU.mult), p, 12)
                link_stat(nc.vector.scalar_tensor_tensor(shift[:, par], mean[:], -1.0, rstd[:, par],
                                                         ALU.mult, ALU.mult), p, 13)
                dve.sem_inc(rstd_ready, 1)

            def set_edges(q_par, j):
                if j == 0:
                    nc.vector.memset(norm[:, q_par, 0], 0.0).then_inc(edged, 1)
                if j == STEPS - 1:
                    nc.vector.memset(norm[:, q_par, OUT * TILES[j] + 1], 0.0).then_inc(edged, 1)

            def differences(q, q_par, j, p, t):
                n = TILES[j]
                dve.wait_ge(normed, q + 1)
                if outside(j):
                    dve.wait_ge(edged, 6 * p + edges_before(j, t))
                g = norm[:, q_par]
                nc.vector.tensor_tensor(diff[:, 0:n].rearrange("p t i c -> p (t i c)"),
                                        g[:, 2:OUT * n + 2].rearrange("p h c -> p (h c)"),
                                        g[:, 0:OUT * n].rearrange("p h c -> p (h c)"), ALU.subtract)
                d12 = g[:, 1:1 + OUT * n].rearrange("p (t i) c -> p t (i c)", i=OUT)[:, :, 0:2 * W]
                d34 = g[:, 1:1 + OUT * n].rearrange("p (t i) c -> p t (i c)", i=OUT)[:, :, 2 * W:4 * W]
                nc.vector.scalar_tensor_tensor(quad[:, 0:n].rearrange("p t i c -> p t (i c)"), d12, -4.0, d34,
                                               ALU.mult, ALU.add).then_inc(diffed, 1)

            def transform(q, j):
                n = TILES[j]
                dve.wait_ge(diffed, q + 1)
                d01 = diff[:, 0:n, 0:2].rearrange("p t i c -> p t (i c)")
                d23 = diff[:, 0:n, 2:4].rearrange("p t i c -> p t (i c)")
                nc.vector.scalar_tensor_tensor(v[:, 0:n, 4:6].rearrange("p t i c -> p t (i c)"), d01, -4.0, d23,
                                               ALU.mult, ALU.add)
                for i, f in ((3, 2.0), (4, -2.0)):
                    nc.vector.scalar_tensor_tensor(v[:, 0:n, SLOT[i]], diff[:, 0:n, 1], f, diff[:, 0:n, 2],
                                                   ALU.mult, ALU.add)
                nc.vector.tensor_tensor(v[:, 0:n, SLOT[1]], quad[:, 0:n, 1], quad[:, 0:n, 0], ALU.add)
                nc.vector.tensor_tensor(v[:, 0:n, SLOT[2]], quad[:, 0:n, 1], quad[:, 0:n, 0], ALU.subtract)\
                  .then_inc(v_ready, 1)

            def low(q, t, j):
                n = TILES[j]
                dve.wait_ge(high_ready, q + 1)
                src = va[:, j % 2, t] if t != R else vr
                view = lambda part_: src[:, part_, 0:n, :, 1:1 + W].rearrange("p t s c -> p (t s) c")
                nc.vector.tensor_tensor(view(1), v[:, 0:n].rearrange("p t s c -> p (t s) c"), view(0),
                                        ALU.subtract).then_inc(low_ready[t], 1)

            def form_halves(k, t, g_par, j):
                n, c = 2 * TILES[j] * W, t // 2
                dve.wait_ge(m13_ready, 3 * k + t + 1 + FREE)
                dve.wait_ge(products, 3 * BANKS * k + BANKS * t + 2)
                m24 = ps[:, BANKS * g_par + 1, 0:n]
                nc.vector.scalar_tensor_tensor(sums[:, g_par, 0:n], m24, unscale[:, c:c + 1], m13[:, g_par, 0:n],
                                               ALU.mult, ALU.add)
                nc.vector.scalar_tensor_tensor(difs[:, g_par, 0:n], m24, minus[:, c:c + 1], m13[:, g_par, 0:n],
                                               ALU.mult, ALU.add).then_inc(halves, 1)

            def combine(k, t, g_par, j, rows):
                n = TILES[j]
                if rows[0] == 0:
                    dve.wait_ge(halves, 3 * k + t + 1 + FREE)
                for row in rows:
                    src, f = (sums, difs)[row % 2], 2.0 ** row
                    one, two = (src[:, g_par, i * n * W:(i + 1) * n * W].rearrange("p (t c) -> p t c", c=W)
                                for i in (0, 1))
                    ins = nc.vector.scalar_tensor_tensor(part[:, 0:n, row], two, f, one, ALU.mult, ALU.add)
                if rows[-1] == OUT - 1:
                    ins.then_inc(combined, 1)

            def add_x(k, t, par, j):
                n = TILES[j]
                dve.wait_ge(combined, 3 * k + t + 1)
                y = xt[:, par, t, FIRST_ROW[j]:FIRST_ROW[j] + OUT * n].rearrange("p h c -> p (h c)")
                nc.vector.tensor_tensor(y, part[:, 0:n].rearrange("p t i c -> p (t i c)"), y, ALU.add)\
                  .then_inc(residual, 1)

            def finish(k, t, g_par, par, j):
                n, c = TILES[j], t // 2
                dve.wait_ge(residual, 3 * k + t + 1)
                dve.wait_ge(products, 3 * BANKS * k + BANKS * t + 3)
                y = xt[:, par, t, FIRST_ROW[j]:FIRST_ROW[j] + OUT * n].rearrange("p (t i) c -> p t i c", i=OUT)
                for i, row in ((0, 0), (1, 3)):
                    m = ps[:, BANKS * g_par + 2, i * n * W:(i + 1) * n * W].rearrange("p (t c) -> p t c", c=W)
                    ins = nc.vector.scalar_tensor_tensor(y[:, :, row], m, unscale[:, c:c + 1], y[:, :, row],
                                                         ALU.mult, ALU.add)
                ins.then_inc(finished, 1)

            nc.vector.memset(ones[:], 1.0).then_inc(cleared, 1)
            for tile_ in (va[:].rearrange("p a b c t s w -> p (a b c t s) w"),
                          vr[:].rearrange("p c t s w -> p (c t s) w")):
                nc.vector.memset(tile_[:, :, 0:WP:WP - 1], 0.0).then_inc(cleared, 1)
            for banks_free in (m13_ready, halves, finished):
                dve.sem_inc(banks_free, FREE)

            dve.wait_ge(rows_loaded, 48)
            for c in (0, 1):
                nc.vector.tensor_reduce(scales[:, 0, c:c + 1], wr[c], AX.X, ALU.max).then_inc(set_dve, 1)
                nc.vector.tensor_reduce(scales[:, 1, c:c + 1], wr[c], AX.X, ALU.min).then_inc(set_dve, 1)
            setup_steps[0] = 4
            dve.wait_ge(set_dve, 4)
            link(nc.vector.scalar_tensor_tensor(scales[:, 2], scales[:, 1], -1.0, scales[:, 0],
                                                ALU.mult, ALU.max))
            link(nc.vector.tensor_scalar(scales[:, 3], scales[:, 2], LEAST, None, ALU.max))
            link(nc.vector.tensor_scalar(scales[:, 4].bitcast(I32), scales[:, 3].bitcast(I32), EXPONENT, None,
                                         ALU.bitwise_and))
            link(nc.vector.tensor_scalar(unscale[:], scales[:, 4], 1.0 / (U_SCALE * V_SCALE), None, ALU.mult))
            link(nc.vector.tensor_scalar(minus[:], unscale[:], -1.0, None, ALU.mult))
            link(nc.vector.reciprocal(scales[:, 5], unscale[:]))
            dve.wait_ge(ident_loaded, 16)
            for c in (0, 1):
                link(nc.vector.tensor_scalar(diag[:, c], ident[:], scales[:, 5, c:c + 1], 1.0 / V_SCALE,
                                             ALU.mult, ALU.mult))
            dve.sem_inc(diag_ready, 1)

            dve.wait_ge(spread_out, 1)
            link(nc.vector.tensor_copy(row_scale[:, 0:P], ps[:, 0, 0:P]))
            link(nc.vector.tensor_copy(row_scale[:, P:CH], ps[:, 1, 0:REST]))

            def scale_weights(c):
                dve.wait_ge(cols_loaded[c], 16 * (c + 1))
                g = wc[c].rearrange("p i k o -> p (i k) o")
                link(nc.vector.tensor_tensor(g, g, row_scale[:].unsqueeze(1).to_broadcast([P, TAPS, CH]), ALU.mult))

            def transform_weights(c):
                g0, g1, g2 = (wc[c][:, i].rearrange("p k o -> p (k o)") for i in range(3))
                to = {i: u[c][:, SLOT[i]] for i in range(1, 5)}
                nc.vector.tensor_tensor(to[1], g0, g2, ALU.add)
                link(nc.vector.scalar_tensor_tensor(to[3], g2, 4.0, g0, ALU.mult, ALU.add))
                nc.vector.tensor_tensor(to[2], to[1], g1, ALU.subtract)
                link(nc.vector.scalar_tensor_tensor(to[4], g1, -2.0, to[3], ALU.mult, ALU.add))
                nc.vector.tensor_tensor(to[1], to[1], g1, ALU.add)
                link(nc.vector.scalar_tensor_tensor(to[3], g1, 2.0, to[3], ALU.mult, ALU.add))
                dve.sem_inc(planes_ready, 1)

            def weights_low_parts(c):
                for n, (high_, low_, planes, f) in enumerate(u_parts(c)):
                    dve.wait_ge(weights_high, UPARTS * c + n + 1)
                    ins = nc.vector.scalar_tensor_tensor(low_, planes, f, high_, ALU.mult, ALU.subtract)
                link(ins)

            scale_weights(0)
            transform_weights(0)
            scale_weights(1)
            channel_moments(0)
            transform_weights(1)
            group_mean(0)
            weights_low_parts(0)
            group_var(0)
            weights_low_parts(1)
            for i in (0, 1):
                mine = slice(i * REST, (i + 1) * REST)
                nc.vector.tensor_copy(us[mine], low_rest[mine, :, i])
            link(nc.vector.tensor_copy(ul[:], low_rest[:, :, KX - 1]))
            dve.sem_inc(weights_ready, 1)
            group_rstd(0, 0)

            for q_, (_, k) in enumerate(PROLOGUE[:2]):
                set_edges(q_, k)
            for q, (t, k) in enumerate(PROLOGUE):
                if q == 0:
                    differences(q, q % 2, k, 0, t)
                else:
                    before, k_before = PROLOGUE[q - 1]
                    dve.wait_ge(low_ready[before], k_before + 1)
                transform(q, k)
                if q + 1 < LEAD:
                    nt, nk = PROLOGUE[q + 1]
                    dve.wait_ge(v_ready, q + 1)
                    if q == 0:
                        set_edges(0, PROLOGUE[2][1])
                    differences(q + 1, (q + 1) % 2, nk, 0, nt)
                low(q, t, k)

            def body(m, last=False):
                for par in (0, 1):
                    final = last and par == 1
                    p, p_par = 2 * m + par + 1, 1 - par
                    for j in range(STEPS):
                        k = 8 * m + 4 * par + j
                        for t in (A, B, R):
                            g_par = (j + t) % 2
                            q, q_par = LEAD + 3 * k + t, (LEAD + j + t) % 2
                            ahead = {A: 1, B: 1, R: 2}[t]
                            jj = (j + ahead) % STEPS
                            of = 2 * m + par + (j + ahead) // STEPS
                            prepares = not (final and j + ahead >= STEPS)
                            form_halves(k, t, g_par, j)
                            if prepares:
                                differences(q, q_par, jj, of, t)
                            nj = j + {A: 1, B: 2, R: 2}[t]
                            if not (final and nj >= STEPS):
                                set_edges(1 - q_par, nj % STEPS)
                            if not final and (j, t) == (2, B):
                                group_var(p)
                            combine(k, t, g_par, j, (0, 1))
                            if prepares:
                                transform(q, jj)
                            combine(k, t, g_par, j, (2, 3))
                            if not final and (j, t) == (1, R):
                                channel_moments(p)
                            if not final and (j, t) == (2, A):
                                group_mean(p)
                            add_x(k, t, par, j)
                            if not final and (j, t) == (2, B):
                                group_rstd(p, p_par)
                            if prepares:
                                low(q, t, jj)
                            finish(k, t, g_par, par, j)

            with dve.Fori(0, PAIRS // 2 - 1) as m:
                body(m)
            body(PAIRS // 2 - 1, last=True)


def kernel(x, L0_conv_weight, L0_conv_bias):
    import concourse.bacc as bacc
    from concourse.bass_utils import run_bass_kernel_spmd

    weight = np.ascontiguousarray(L0_conv_weight)
    arrays = {
        "x": np.ascontiguousarray(x),
        "w_rows": weight,
        "w_cols": np.ascontiguousarray(weight.reshape(CH, CH, 3, KX).transpose(1, 2, 3, 0)),
        "bias": np.ascontiguousarray(L0_conv_bias).reshape(CH, 1),
        "matrices": group_matrices(),
        "identity": np.eye(P, dtype=np.float32),
    }
    nc = bacc.Bacc("TRN2", target_bir_lowering=False, num_devices=1)
    args = [nc.dram_tensor(name, a.shape, F32, kind="ExternalInput").ap() for name, a in arrays.items()]
    out = nc.dram_tensor("out", (IMAGES, CH, H, W), F32, kind="ExternalOutput").ap()
    preact_conv(nc, *args, out)
    r = run_bass_kernel_spmd(nc, [arrays], core_ids=[0])
    return r.results[0]["out"]
```

```python
from contextlib import ExitStack

import numpy as np

import concourse.bass as bass
from concourse import mybir

F32 = mybir.dt.float32
F16 = mybir.dt.float16
BF16 = mybir.dt.bfloat16
I32 = mybir.dt.int32
ALU = mybir.AluOpType
ACT = mybir.ActivationFunctionType
AX = mybir.AxisListType

P = 128
IMAGES, CH, H, W = 32, 192, 56, 56
REST = CH - P
GROUPS, EPS = 32, 1e-5
PER_GROUP = CH // GROUPS
KX = 3
TAPS = 3 * KX
PAIRS = IMAGES // 2

OUT = 4
POINTS = OUT + 2
TILES = (4, 4, 4, 2)
STEPS = len(TILES)
FIRST_ROW = [OUT * sum(TILES[:j]) for j in range(STEPS)]
MAXT = max(TILES)
WP = W + 2
assert OUT * sum(TILES) == H

SLOT = {1: 0, 3: 1, 2: 2, 4: 3, 0: 4, 5: 5}
BANKS = POINTS // 2

A, B, R = 0, 1, 2
V_SCALE = 32.0
U_SCALE = 2.0 ** 14
LEAST = 2.0 ** -100
EXPONENT = 0x7F800000

PROLOGUE = [(R, 0), (A, 0), (B, 0), (R, 1)]
LEAD = len(PROLOGUE)


def group_matrices():
    a = np.arange(P) // PER_GROUP
    r = (P + np.arange(P) % REST) // PER_GROUP
    mats = [a[:, None] == a, r[:, None] == a, a[:, None] == r, r[:, None] == r]
    return (np.stack(mats, axis=1) / PER_GROUP).astype(np.float32)


AA, RA, AR, RR = range(4)


def preact_conv(nc, x, w_rows, w_cols, bias, matrices, identity, out):
    with ExitStack() as ctx:
        def sb(name, shape, dt=F32):
            return ctx.enter_context(nc.sbuf_tensor(name, shape, dt))

        def sem(name):
            return ctx.enter_context(nc.semaphore(name))

        xt = sb("xt", [P, 2, 3, H, W])
        norm = sb("norm", [P, 2, OUT * MAXT + 2, W])
        diff = sb("diff", [P, MAXT, OUT, W])
        quad = sb("quad", [P, MAXT, 2, W])
        v = sb("v", [P, MAXT, POINTS, W])
        va = sb("va", [P, 2, 2, 2, MAXT, POINTS, WP], F16)
        vr = sb("vr", [P, 2, MAXT, POINTS, WP], F16)
        st = sb("st", [P, 2, 2, 2, MAXT, POINTS, WP], F16)
        prod = sb("prod", [P, 2, BANKS, 2 * MAXT * W])
        sums = sb("sums", [P, 2, 2 * MAXT * W])
        difs = sb("difs", [P, 2, 2 * MAXT * W])
        part = sb("part", [P, MAXT, OUT, W])

        ua = sb("ua", [P, 2, POINTS, KX, CH], F16)
        ur = sb("ur", [P, POINTS, KX, CH], F16)
        ul = sb("ul", [P, POINTS, CH], F16)
        us = sb("us", [P, POINTS, CH], F16)

        mats = sb("mats", [P, 4, P])
        ident = sb("ident", [P, P])
        ones = sb("ones", [P, P])
        zeros = sb("zeros", [P, W])
        biases = sb("biases", [P, 2])
        unscale = sb("unscale", [P, 2])
        scales = sb("scales", [P, 4, 2])
        diag = sb("diag", [P, 2, P])
        row_scale = sb("row_scale", [P, CH])

        unread = sb("unread", [P, H * W], BF16)
        total = sb("total", [P, 3])
        neg_mean = sb("neg_mean", [P, 3])
        squares = sb("squares", [P, 3])
        spread = sb("spread", [P, 3])
        dev = sb("dev", [P, 3])
        neg_group = sb("neg_group", [P, 3])
        group_mask = sb("group_mask", [P, 4])
        split_mean = sb("split_mean", [P, 4])
        split_spread = sb("split_spread", [P, 4])
        mean4 = sb("mean4", [P, 4])
        picked = sb("picked", [P, 4])
        rstd4 = sb("rstd4", [P, 4])
        ve = sb("ve", [P, 4])
        sd = sb("sd", [P, 4])
        r0 = sb("r0", [P, 4])
        r1 = sb("r1", [P, 4])
        half = sb("half", [P, 4])
        three = sb("three", [P, 4])
        zero = sb("zero", [P, 2])
        per_channel = sb("per_channel", [P, 3])
        rstd = sb("rstd", [P, 2, 3])
        shift = sb("shift", [P, 2, 3])

        flat = xt[:, 1, :, :, :].rearrange("p u h w -> p (u h w)")
        WIDE = TAPS * CH
        wr = [flat[:, i * WIDE:(i + 1) * WIDE] for i in (0, 1)]
        wc = [flat[:, i * WIDE:(i + 1) * WIDE].rearrange("p (i k o) -> p i k o", i=3, k=KX)
              for i in (2, 3)]
        PLANE = KX * CH
        u = [flat[:, at:at + 4 * PLANE].rearrange("p (s n) -> p s n", s=4) for at in (0, 4 * WIDE)]
        low_rest = st[:, 1].rearrange("p i a t s c -> p (i a t s c)")[:, 0:POINTS * PLANE]\
            .rearrange("p (s k o) -> p s k o", s=POINTS, k=KX)

        ps = ctx.enter_context(nc.psum_tensor("ps", [P, 8, 512], F32))
        STAT = 2 * BANKS

        x_loaded = [[sem(f"x_loaded{p}{t}") for t in range(3)] for p in range(2)]
        rows_loaded = sem("rows_loaded")
        cols_loaded = [sem("cols_loaded0"), sem("cols_loaded1")]
        ident_loaded = sem("ident_loaded")
        const_loaded = sem("const_loaded")
        cleared = sem("cleared")
        set_dve = sem("set_dve")
        diag_ready = sem("diag_ready")
        spread_out = sem("spread_out")
        weights_summed = sem("weights_summed")
        planes_ready = sem("planes_ready")
        weights_high = sem("weights_high")
        weights_ready = sem("weights_ready")
        summed = sem("summed")
        means_split = sem("means_split")
        moments_out = sem("moments_out")
        means_ready = sem("means_ready")
        spread_ready = sem("spread_ready")
        var_ready = sem("var_ready")
        sd_ready = sem("sd_ready")
        inverse_ready = sem("inverse_ready")
        stat_pool = sem("stat_pool")
        pool_set = sem("pool_set")
        rstd_ready = sem("rstd_ready")
        sp_passed = sem("sp_passed")
        normed = sem("normed")
        diffed = sem("diffed")
        v_ready = sem("v_ready")
        high_ready = sem("high_ready")
        low_ready = [sem(f"low_ready{t}") for t in range(3)]
        stacked = [[sem(f"stacked{p}{i}") for i in (0, 1)] for p in (0, 1)]
        products = sem("products")
        copied = [sem(f"copied{b}") for b in range(BANKS)]
        halves = sem("halves")
        combined = sem("combined")
        residual = sem("residual")
        finished = sem("finished")
        y_stored = [sem("y_stored0"), sem("y_stored1")]

        STACK_INC = 4 * 16
        UNIT_INC = [16, 16, 32]
        PAIR_STORED = STEPS * sum(UNIT_INC)
        SUMS, EXTRA = 7, 2
        FREE = 2
        CREDIT = 16

        def u_parts(c):
            high_, low_ = (ua[:, 0], ua[:, 1]) if c == 0 else (ur[:], low_rest)
            g0, g2 = (wc[c][:, i].rearrange("p k o -> p (k o)") for i in (0, 2))
            for slots, planes, f in ((slice(0, 4, 2), u[c][:, 0:4:2], -1.0 / 6),
                                     (slice(1, 4, 2), u[c][:, 1:4:2], 1.0 / 24),
                                     (SLOT[0], g0, 0.25), (SLOT[5], g2, 1.0)):
                to = "p s k o -> p s (k o)" if isinstance(slots, slice) else "p k o -> p (k o)"
                yield high_[:, slots].rearrange(to), low_[:, slots].rearrange(to), planes, f

        block = ctx.enter_context(nc.Block())

        @block.sync
        def _(sp):
            def load(first, par):
                for t in (A, B):
                    sp.dma_start(xt[:, par, t], x[bass.ds(first + t, 1), 0:P].rearrange("n c h w -> (n c) h w"))\
                      .then_inc(x_loaded[par][t], 16)
                for i in (0, 1):
                    sp.dma_start(xt[i * REST:(i + 1) * REST, par, R],
                                 x[bass.ds(first + i, 1), P:CH].rearrange("n c h w -> (n c) h w"))\
                      .then_inc(x_loaded[par][R], 16)

            def store(first, par, t, j):
                rows = slice(FIRST_ROW[j], FIRST_ROW[j] + OUT * TILES[j])
                if t != R:
                    sp.dma_start(out[bass.ds(first + t, 1), 0:P, rows].rearrange("n c h w -> (n c) h w"),
                                 xt[:, par, t, rows]).then_inc(y_stored[par], 16)
                else:
                    for i in (0, 1):
                        sp.dma_start(out[bass.ds(first + i, 1), P:CH, rows].rearrange("n c h w -> (n c) h w"),
                                     xt[i * REST:(i + 1) * REST, par, t, rows]).then_inc(y_stored[par], 16)

            def stack(j, sp_):
                n = TILES[j] * POINTS * WP
                for i in (0, 1):
                    mine = slice(i * REST, (i + 1) * REST)
                    high = vr[mine, 0].rearrange("p t s c -> p (t s c)")
                    low = vr[mine, 1].rearrange("p t s c -> p (t s c)")
                    s1 = st[:, sp_, i, 0].rearrange("p t s c -> p (t s c)")
                    s2 = st[:, sp_, i, 1].rearrange("p t s c -> p (t s c)")
                    sp.dma_start(s1[0:REST, 0:n], high[:, 0:n]).then_inc(stacked[sp_][i], 16)
                    sp.dma_start(s1[REST:P, 0:n], low[:, 0:n]).then_inc(stacked[sp_][i], 16)
                    sp.dma_start(s2[0:REST, 0:n], high[:, 0:n]).then_inc(stacked[sp_][i], 16)
                    sp.dma_start(s2[REST:P, 0:n - 1], high[:, 1:n]).then_inc(stacked[sp_][i], 16)

            sp.dma_start(wr[0], w_rows[0:P]).then_inc(rows_loaded, 16)
            for i in (0, 1):
                sp.dma_start(wr[1][i * REST:(i + 1) * REST], w_rows[P:CH]).then_inc(rows_loaded, 16)
            sp.dma_start(ident[:], identity).then_inc(ident_loaded, 16)
            sp.dma_start(wc[0], w_cols[0:P]).then_inc(cols_loaded[0], 16)
            load(0, 0)
            for i in (0, 1):
                sp.dma_start(wc[1][i * REST:(i + 1) * REST], w_cols[P:CH]).then_inc(cols_loaded[1], 16)
            sp.dma_start(mats[:], matrices).then_inc(const_loaded, 16)
            sp.dma_start(biases[:, 0:1], bias[0:P]).then_inc(const_loaded, 16)
            for i in (0, 1):
                sp.dma_start(biases[i * REST:(i + 1) * REST, 1:2], bias[P:CH]).then_inc(const_loaded, 16)
            for par in (0, 1):
                sp.sem_inc(y_stored[par], CREDIT)
            for k in (0, 1):
                sp.wait_ge(low_ready[R], k + 1)
                stack(k, k % 2)
            sp.wait_ge(weights_ready, 1)

            def body(m, last=False):
                for par in (0, 1):
                    final = last and par == 1
                    first = 4 * m + 2 * par
                    if not final:
                        sp.wait_ge(y_stored[1 - par], PAIR_STORED * (m + par) + CREDIT)
                        sp.sem_inc(sp_passed, 1)
                        load(first + 2, 1 - par)
                    for j in range(STEPS):
                        k = 8 * m + 4 * par + j
                        for t in (A, B, R):
                            sp.wait_ge(finished, 3 * k + t + 1 + FREE)
                            sp.sem_inc(sp_passed, 1)
                            store(first, par, t, j)
                        if not (final and j >= 2):
                            sp.wait_ge(low_ready[R], k + 3)
                            sp.sem_inc(sp_passed, 1)
                            sp.wait_ge(products, 3 * BANKS * (k + 1))
                            stack((j + 2) % STEPS, j % 2)

            with sp.Fori(0, PAIRS // 2 - 1) as m:
                body(m)
            body(PAIRS // 2 - 1, last=True)
            for par in (0, 1):
                sp.wait_ge(y_stored[par], PAIR_STORED * PAIRS // 2 + CREDIT)

        @block.tensor
        def _(pe):
            def average(rnd):
                src = (split_mean, split_spread)[rnd]
                for at, mats_ in ((slice(0, 2), (AA, RA)), (slice(2, 4), (AR, RR))):
                    for i, mat in enumerate(mats_):
                        mm = nc.tensor.matmul(ps[:, STAT + rnd, at], mats[:, mat], src[:, 2 * i:2 * i + 2],
                                              start=(i == 0), stop=(i == 1))
                mm.then_inc(moments_out, 1)

            def bank_of_products(b, g_par, t, j):
                n, kp = TILES[j], j % 2
                images = (t,) if t != R else (0, 1)
                couts = slice(0, P) if t != R else slice(P, CH)
                for s in (2 * b, 2 * b + 1):
                    at_cols = slice((s % 2) * n * W, (s % 2 + 1) * n * W)

                    def parts(i, part, kx):
                        return va[:, kp, i, part, 0:n, s, kx:kx + W]

                    def stacks(i, which, kx):
                        return st[:, kp, i, which, 0:n, s, kx:kx + W]

                    terms = []
                    for kx in range(KX):
                        terms += [(ua[:, 0, s, kx, couts], parts, 0, kx),
                                  (ua[:, 1, s, kx, couts], parts, 0, kx),
                                  (ua[:, 0, s, kx, couts], parts, 1, kx)]
                    terms += [(ur[:, s, kx, couts], stacks, 0, kx) for kx in range(KX)]
                    terms += [(ul[:, s, couts], stacks, 0, KX - 1), (us[:, s, couts], stacks, 1, 0)]
                    for i_term, (lhs, tile_of, which, kx) in enumerate(terms):
                        for i in images:
                            at = slice(0, P) if t != R else slice(i * REST, (i + 1) * REST)
                            mm = nc.tensor.matmul(ps[at, BANKS * g_par + b, at_cols], lhs, tile_of(i, which, kx),
                                                  start=(i_term == 0), stop=(i_term == len(terms) - 1))
                mm.then_inc(products, 1)

            pe.wait_ge(cleared, 1)
            pe.wait_ge(diag_ready, 1)
            nc.tensor.matmul(ps[:, 0, 0:P], ones[:], diag[:, 0], start=True, stop=True)
            nc.tensor.matmul(ps[:, 1, 0:REST], ones[0:REST], diag[0:REST, 1, 0:REST], start=True, stop=True)\
              .then_inc(spread_out, 1)
            pe.wait_ge(const_loaded, 64)
            pe.wait_ge(means_split, 1)
            average(0)
            pe.wait_ge(spread_ready, 1)
            average(1)
            pe.wait_ge(weights_ready, 1)

            def body(n, last=False):
                for j in range(STEPS):
                    k = STEPS * n + j
                    for t in (A, B, R):
                        g_par = (j + t) % 2
                        if t != R:
                            pe.wait_ge(low_ready[t], k + 1)
                            pe.wait_ge(stacked[j % 2][t], STACK_INC * (2 * n + j // 2 + 1))
                        for b in range(BANKS):
                            if (j, t, b) == (2, A, 0) and not last:
                                pe.wait_ge(means_split, n + 2)
                                average(0)
                            if (j, t, b) == (2, B, 2) and not last:
                                pe.wait_ge(spread_ready, n + 2)
                                average(1)
                            pe.wait_ge(copied[b], 3 * k + t + 1)
                            bank_of_products(b, g_par, t, j)

            with pe.Fori(0, PAIRS - 1) as n:
                body(n)
            body(PAIRS - 1, last=True)

        @block.scalar
        def _(act):
            def x_flat(par, t):
                return xt[:, par, t].rearrange("p h w -> p (h w)")

            def sum_x(p, par, t, m):
                act.wait_ge(x_loaded[par][t], UNIT_INC[t] * (m + 1))
                act.wait_ge(summed, SUMS * p + EXTRA + t)
                nc.scalar.activation(unread[:], x_flat(par, t), ACT.Copy, accum_out=total[:, t:t + 1])\
                  .then_inc(summed, 1)

            def negate_means(p):
                act.wait_ge(summed, SUMS * p + EXTRA + 3)
                nc.scalar.mul(neg_mean[:], total[:], -1.0 / (H * W)).then_inc(summed, 1)

            def sum_squares(p, par, t):
                act.wait_ge(summed, SUMS * p + EXTRA + 4 + t)
                nc.scalar.activation(unread[:], x_flat(par, t), ACT.Square, bias=neg_mean[:, t:t + 1],
                                     accum_out=squares[:, t:t + 1]).then_inc(summed, 1)

            def deviation(p):
                act.wait_ge(var_ready, p + 1)
                nc.scalar.activation(sd[:], ve[:], ACT.Sqrt).then_inc(sd_ready, 1)

            def normalise(q_par, t, par, j):
                first, n = FIRST_ROW[j] - 1, OUT * TILES[j] + 2
                top, bottom = max(first, 0), min(first + n, H)
                for row in ([0] if top > first else []) + ([n - 1] if bottom < first + n else []):
                    nc.scalar.copy(norm[:, q_par, row], zeros[:])
                nc.scalar.activation(norm[:, q_par, top - first:bottom - first], xt[:, par, t, top:bottom],
                                     ACT.Identity, bias=shift[:, par, t:t + 1], scale=rstd[:, par, t:t + 1])\
                  .then_inc(normed, 1)

            def high(q, t, j):
                n = TILES[j]
                act.wait_ge(v_ready, q + 1)
                to = va[:, j % 2, t, 0, 0:n] if t != R else vr[:, 0, 0:n]
                nc.scalar.copy(to[:, :, :, 1:1 + W].rearrange("p t s c -> p (t s) c"),
                               v[:, 0:n].rearrange("p t s c -> p (t s) c")).then_inc(high_ready, 1)

            def first_statistics(t):
                act.wait_ge(x_loaded[0][t], UNIT_INC[t])
                if t != A:
                    act.wait_ge(summed, 3 * t)
                nc.scalar.activation(unread[:], x_flat(0, t), ACT.Copy, accum_out=total[:, t:t + 1])\
                  .then_inc(summed, 1)
                act.wait_ge(summed, 3 * t + 1)
                nc.scalar.mul(neg_mean[:, t:t + 1], total[:, t:t + 1], -1.0 / (H * W)).then_inc(summed, 1)
                act.wait_ge(summed, 3 * t + 2)
                nc.scalar.activation(unread[:], x_flat(0, t), ACT.Square, bias=neg_mean[:, t:t + 1],
                                     accum_out=squares[:, t:t + 1]).then_inc(summed, 1)

            act.wait_ge(cleared, 1)
            nc.scalar.activation(sd[:, 0:1], ones[:, 0:1], ACT.Sqrt)
            act.wait_ge(rows_loaded, 48)
            for c in (0, 1):
                nc.scalar.activation(wr[c], wr[c], ACT.Abs, accum_out=scales[:, 0, c:c + 1])\
                  .then_inc(weights_summed, 1)
            for t in (A, B, R):
                first_statistics(t)
            act.wait_ge(planes_ready, 1)
            for high_, _, planes, f in u_parts(1):
                nc.scalar.mul(high_, planes, f).then_inc(weights_high, 1)
            deviation(0)
            act.wait_ge(cleared, 4)
            act.wait_ge(const_loaded, 64)
            act.wait_ge(rstd_ready, 1)
            normalise(0, R, 0, 0)
            following = PROLOGUE[1:] + [(A, 1)]
            for q, (t, k) in enumerate(PROLOGUE):
                if q:
                    act.wait_ge(v_ready, q)
                nt, nk = following[q]
                normalise((q + 1) % 2, nt, 0, nk)
                if (t, k) == (R, 1):
                    for i in (0, 1):
                        act.wait_ge(stacked[0][i], STACK_INC)
                high(q, t, k)

            def copy_bank(b, k, j, t):
                n, g_par, c = 2 * TILES[j] * W, (j + t) % 2, t // 2
                act.wait_ge(products, BANKS * (3 * k + t) + b + 1)
                act.wait_ge((halves, finished)[b // 2], 3 * k + t + 1)
                nc.scalar.mul(prod[:, g_par, b, 0:n], ps[:, BANKS * g_par + b, 0:n], unscale[:, c:c + 1])\
                  .then_inc(copied[b], 1)

            act.wait_ge(weights_ready, 1)
            for b in (0, 1):
                copy_bank(b, 0, 0, A)

            def body(m, last=False):
                for par in (0, 1):
                    final = last and par == 1
                    p, p_par = 2 * m + par + 1, 1 - par
                    for j in range(STEPS):
                        k = 8 * m + 4 * par + j
                        for t in (A, B, R):
                            late = (j, t) == (1, R)
                            if not late:
                                copy_bank(2, k, j, t)
                            if (j, t) == (2, B) and not final:
                                deviation(p)
                            ahead = {A: 1, B: 1, R: 2}[t]
                            if not (final and j + ahead >= STEPS):
                                if t == R:
                                    for i in (0, 1):
                                        act.wait_ge(stacked[(j + 1) % 2][i],
                                                    STACK_INC * (4 * m + 2 * par + (j + 1) // 2 + 1))
                                high(LEAD + 3 * k + t, t, (j + ahead) % STEPS)
                            if late:
                                copy_bank(2, k, j, t)
                            for b in (0, 1):
                                if t != R:
                                    copy_bank(b, k, j, t + 1)
                                elif not (final and j == STEPS - 1):
                                    copy_bank(b, k + 1, (j + 1) % STEPS, A)
                            nt, nj = (t + 1) % 3, j + {A: 1, B: 2, R: 2}[t]
                            if (j, t) == (2, B) and not final:
                                act.wait_ge(rstd_ready, p + 1)
                            if not (final and nj >= STEPS):
                                normalise((LEAD + j + t + 1) % 2, nt, (par + nj // STEPS) % 2, nj % STEPS)
                            if final:
                                continue
                            if (j, t) == (0, B):
                                sum_x(p, p_par, A, m + par)
                            if (j, t) == (0, R):
                                sum_x(p, p_par, B, m + par)
                                sum_x(p, p_par, R, m + par)
                            if (j, t) == (1, A):
                                negate_means(p)
                                sum_squares(p, p_par, A)
                            if (j, t) == (1, B):
                                sum_squares(p, p_par, B)
                                sum_squares(p, p_par, R)

            with act.Fori(0, PAIRS // 2 - 1) as m:
                body(m)
            body(PAIRS // 2 - 1, last=True)

        @block.gpsimd
        def _(pool):
            CHAIN = 12

            def link(ins, p, i):
                ins.then_inc(stat_pool, 1)
                pool.wait_ge(stat_pool, CHAIN * p + i)

            def split(to, src):
                nc.gpsimd.tensor_tensor(to[:, 0:3], src[:], group_mask[:, 0:3], ALU.mult)
                return nc.gpsimd.tensor_tensor(to[:, 3:4], src[:, 2:3], group_mask[:, 3:4], ALU.mult)

            def pick(to, src, p, i):
                link(nc.gpsimd.tensor_tensor(picked[:], src[:], group_mask[:], ALU.mult), p, i)
                nc.gpsimd.tensor_tensor(to[:, 0:2], picked[:, 0:2], zero[:], ALU.add)
                link(nc.gpsimd.tensor_tensor(to[:, 2:3], picked[:, 2:3], picked[:, 3:4], ALU.add), p, i + 1)

            def split_means(p, steps_before):
                pool.wait_ge(summed, steps_before)
                split(split_mean, neg_mean).then_inc(means_split, 1)

            def group_spread(p):
                pool.wait_ge(means_ready, p + 1)
                pick(neg_group, mean4, p, 1)
                link(nc.gpsimd.tensor_tensor(dev[:], neg_mean[:], neg_group[:], ALU.subtract), p, 3)
                link(nc.gpsimd.tensor_tensor(dev[:], dev[:], dev[:], ALU.mult), p, 4)
                pool.wait_ge(summed, SUMS * (p + 1) + EXTRA)
                link(nc.gpsimd.tensor_tensor(spread[:], squares[:], per_channel[:], ALU.mult), p, 5)
                link(nc.gpsimd.tensor_tensor(spread[:], spread[:], dev[:], ALU.add), p, 6)
                split(split_spread, spread).then_inc(spread_ready, 1)

            def group_rstd(p, par):
                pool.wait_ge(inverse_ready, p + 1)
                nc.gpsimd.tensor_tensor(r1[:], ve[:], r0[:], ALU.mult)
                link(nc.gpsimd.tensor_scalar(half[:], r0[:], 0.5 * V_SCALE, None, ALU.mult), p, 7)
                link(nc.gpsimd.tensor_tensor(r1[:], r1[:], r0[:], ALU.mult), p, 8)
                link(nc.gpsimd.tensor_tensor(r1[:], three[:], r1[:], ALU.subtract), p, 9)
                link(nc.gpsimd.tensor_tensor(rstd4[:], half[:], r1[:], ALU.mult), p, 10)
                pick(rstd[:, par], rstd4, p, 11)
                nc.gpsimd.tensor_tensor(shift[:, par], neg_group[:], rstd[:, par], ALU.mult).then_inc(rstd_ready, 1)

            def statistics(p, par, steps_before=None):
                split_means(p, steps_before or SUMS * p + EXTRA + 4)
                group_spread(p)
                group_rstd(p, par)

            for tile_, value in ((three, 3.0), (zero, 0.0), (per_channel, 1.0 / (H * W))):
                nc.gpsimd.memset(tile_[:], value).then_inc(pool_set, 1)
            pool.wait_ge(pool_set, 3)
            pool.wait_ge(cleared, 6)
            statistics(0, 0, steps_before=SUMS + EXTRA - 1)
            with pool.Fori(0, PAIRS // 2 - 1) as m:
                statistics(2 * m + 1, 1)
                statistics(2 * m + 2, 0)
            statistics(PAIRS - 1, 1)

        @block.vector
        def _(dve):
            setup_steps = [0]

            def link(ins):
                setup_steps[0] += 1
                ins.then_inc(set_dve, 1)
                dve.wait_ge(set_dve, setup_steps[0])

            def group_means(p):
                dve.wait_ge(moments_out, 2 * p + 1)
                nc.vector.tensor_copy(mean4[:], ps[:, STAT, 0:4]).then_inc(means_ready, 1)

            def group_variances(p):
                dve.wait_ge(moments_out, 2 * p + 2)
                nc.vector.tensor_scalar(ve[:], ps[:, STAT + 1, 0:4], EPS, None, ALU.add).then_inc(var_ready, 1)

            def group_inverse(p):
                dve.wait_ge(sd_ready, p + 1)
                nc.vector.reciprocal(r0[:], sd[:]).then_inc(inverse_ready, 1)

            def differences(q, q_par, j):
                n = TILES[j]
                dve.wait_ge(normed, q + 1)
                g = norm[:, q_par]
                nc.vector.tensor_tensor(diff[:, 0:n].rearrange("p t i c -> p (t i c)"),
                                        g[:, 2:OUT * n + 2].rearrange("p h c -> p (h c)"),
                                        g[:, 0:OUT * n].rearrange("p h c -> p (h c)"), ALU.subtract)
                d12 = g[:, 1:1 + OUT * n].rearrange("p (t i) c -> p t (i c)", i=OUT)[:, :, 0:2 * W]
                d34 = g[:, 1:1 + OUT * n].rearrange("p (t i) c -> p t (i c)", i=OUT)[:, :, 2 * W:4 * W]
                nc.vector.scalar_tensor_tensor(quad[:, 0:n].rearrange("p t i c -> p t (i c)"), d12, -4.0, d34,
                                               ALU.mult, ALU.add).then_inc(diffed, 1)

            def transform(q, j):
                n = TILES[j]
                dve.wait_ge(diffed, q + 1)
                d01 = diff[:, 0:n, 0:2].rearrange("p t i c -> p t (i c)")
                d23 = diff[:, 0:n, 2:4].rearrange("p t i c -> p t (i c)")
                nc.vector.scalar_tensor_tensor(v[:, 0:n, 4:6].rearrange("p t i c -> p t (i c)"), d01, -4.0, d23,
                                               ALU.mult, ALU.add)
                for i, f in ((3, 2.0), (4, -2.0)):
                    nc.vector.scalar_tensor_tensor(v[:, 0:n, SLOT[i]], diff[:, 0:n, 1], f, diff[:, 0:n, 2],
                                                   ALU.mult, ALU.add)
                nc.vector.tensor_tensor(v[:, 0:n, SLOT[1]], quad[:, 0:n, 1], quad[:, 0:n, 0], ALU.add)
                nc.vector.tensor_tensor(v[:, 0:n, SLOT[2]], quad[:, 0:n, 1], quad[:, 0:n, 0], ALU.subtract)\
                  .then_inc(v_ready, 1)

            def low(q, t, j):
                n = TILES[j]
                dve.wait_ge(high_ready, q + 1)
                src = va[:, j % 2, t] if t != R else vr
                view = lambda part_: src[:, part_, 0:n, :, 1:1 + W].rearrange("p t s c -> p (t s) c")
                nc.vector.tensor_tensor(view(1), v[:, 0:n].rearrange("p t s c -> p (t s) c"), view(0),
                                        ALU.subtract).then_inc(low_ready[t], 1)

            def form_halves(k, t, g_par, j):
                n = 2 * TILES[j] * W
                for b in (0, 1):
                    dve.wait_ge(copied[b], 3 * k + t + 1 + FREE)
                m13, m24 = prod[:, g_par, 0, 0:n], prod[:, g_par, 1, 0:n]
                nc.vector.tensor_tensor(sums[:, g_par, 0:n], m13, m24, ALU.add)
                nc.vector.tensor_tensor(difs[:, g_par, 0:n], m13, m24, ALU.subtract).then_inc(halves, 1)

            def combine(k, t, g_par, j, rows):
                n = TILES[j]
                if rows[0] == 0:
                    dve.wait_ge(halves, 3 * k + t + 1 + FREE)
                for row in rows:
                    if row == 2:
                        ins.then_inc(combined, 1)
                    src, f = (sums, difs)[row % 2], 2.0 ** row
                    one, two = (src[:, g_par, i * n * W:(i + 1) * n * W].rearrange("p (t c) -> p t c", c=W)
                                for i in (0, 1))
                    ins = nc.vector.scalar_tensor_tensor(part[:, 0:n, row], two, f, one, ALU.mult, ALU.add)
                if rows[-1] == OUT - 1:
                    ins.then_inc(combined, 1)

            def add_x(k, t, par, j):
                n = TILES[j]
                y = xt[:, par, t, FIRST_ROW[j]:FIRST_ROW[j] + OUT * n].rearrange("p (t i) c -> p t (i c)", i=OUT)
                p_ = part[:, 0:n].rearrange("p t i c -> p t (i c)")
                for half, at in enumerate((slice(0, 2 * W), slice(2 * W, 4 * W))):
                    dve.wait_ge(combined, 2 * (3 * k + t) + half + 1)
                    ins = nc.vector.scalar_tensor_tensor(y[:, :, at], p_[:, :, at], biases[:, t // 2:t // 2 + 1],
                                                         y[:, :, at], ALU.add, ALU.add)
                ins.then_inc(residual, 1)

            def finish(k, t, g_par, par, j):
                n = TILES[j]
                dve.wait_ge(residual, 3 * k + t + 1)
                dve.wait_ge(copied[2], 3 * k + t + 1 + FREE)
                y = xt[:, par, t, FIRST_ROW[j]:FIRST_ROW[j] + OUT * n]\
                    .rearrange("p (t i) c -> p t i c", i=OUT)[:, :, 0:OUT:OUT - 1]
                m05 = prod[:, g_par, 2, 0:2 * n * W].rearrange("p (i t c) -> p t i c", i=2, c=W)
                nc.vector.tensor_tensor(y, m05, y, ALU.add).then_inc(finished, 1)

            nc.vector.memset(ones[:], 1.0).then_inc(cleared, 1)
            nc.vector.memset(zeros[:], 0.0).then_inc(cleared, 1)
            for tile_ in (va[:].rearrange("p a b c t s w -> p (a b c t s) w"),
                          vr[:].rearrange("p c t s w -> p (c t s) w")):
                nc.vector.memset(tile_[:, :, 0:WP:WP - 1], 0.0).then_inc(cleared, 1)
            nc.vector.memset(group_mask[:], 1.0).then_inc(cleared, 1)
            dve.wait_ge(cleared, 5)
            nc.vector.memset(group_mask[REST:P, 2:3], 0.0)
            nc.vector.memset(group_mask[0:REST, 3:4], 0.0).then_inc(cleared, 1)
            for free in copied + [halves, finished]:
                dve.sem_inc(free, FREE)

            dve.wait_ge(weights_summed, 2)
            link(nc.vector.tensor_scalar(scales[:, 1], scales[:, 0], LEAST, None, ALU.max))
            link(nc.vector.tensor_scalar(scales[:, 2].bitcast(I32), scales[:, 1].bitcast(I32), EXPONENT, None,
                                         ALU.bitwise_and))
            link(nc.vector.tensor_scalar(unscale[:], scales[:, 2], 1.0 / (U_SCALE * V_SCALE), None, ALU.mult))
            link(nc.vector.reciprocal(scales[:, 3], unscale[:]))
            dve.wait_ge(ident_loaded, 16)
            for c in (0, 1):
                link(nc.vector.tensor_scalar(diag[:, c], ident[:], scales[:, 3, c:c + 1], 1.0 / V_SCALE,
                                             ALU.mult, ALU.mult))
            dve.sem_inc(diag_ready, 1)

            dve.wait_ge(spread_out, 1)
            link(nc.vector.tensor_copy(row_scale[:, 0:P], ps[:, 0, 0:P]))
            link(nc.vector.tensor_copy(row_scale[:, P:CH], ps[:, 1, 0:REST]))

            def scale_weights(c):
                dve.wait_ge(cols_loaded[c], 16 * (c + 1))
                g = wc[c].rearrange("p i k o -> p (i k) o")
                link(nc.vector.tensor_tensor(g, g, row_scale[:].unsqueeze(1).to_broadcast([P, TAPS, CH]), ALU.mult))

            def transform_weights(c):
                g0, g1, g2 = (wc[c][:, i].rearrange("p k o -> p (k o)") for i in range(3))
                to = {i: u[c][:, SLOT[i]] for i in range(1, 5)}
                nc.vector.tensor_tensor(to[1], g0, g2, ALU.add)
                link(nc.vector.scalar_tensor_tensor(to[3], g2, 4.0, g0, ALU.mult, ALU.add))
                nc.vector.tensor_tensor(to[2], to[1], g1, ALU.subtract)
                link(nc.vector.scalar_tensor_tensor(to[4], g1, -2.0, to[3], ALU.mult, ALU.add))
                if c == 1:
                    group_means(0)
                nc.vector.tensor_tensor(to[1], to[1], g1, ALU.add)
                link(nc.vector.scalar_tensor_tensor(to[3], g1, 2.0, to[3], ALU.mult, ALU.add))

            def weights_low_parts(c):
                for n, (high_, low_, planes, f) in enumerate(u_parts(c)):
                    if c == 1:
                        dve.wait_ge(weights_high, n + 1)
                    ins = nc.vector.scalar_tensor_tensor(low_, planes, f, high_, ALU.mult, ALU.subtract)
                    if (c, n) == (1, 0):
                        group_variances(0)
                        group_inverse(0)
                link(ins)

            scale_weights(0)
            transform_weights(0)
            for high_, _, planes, f in u_parts(0):
                ins = nc.vector.tensor_scalar(high_, planes, f, None, ALU.mult)
            link(ins)
            weights_low_parts(0)
            scale_weights(1)
            transform_weights(1)
            dve.sem_inc(planes_ready, 1)
            weights_low_parts(1)
            for i in (0, 1):
                mine = slice(i * REST, (i + 1) * REST)
                nc.vector.tensor_copy(us[mine], low_rest[mine, :, i])
            link(nc.vector.tensor_copy(ul[:], low_rest[:, :, KX - 1]))
            dve.sem_inc(weights_ready, 1)

            for q, (t, k) in enumerate(PROLOGUE):
                if q == 0:
                    differences(q, q % 2, k)
                else:
                    before, k_before = PROLOGUE[q - 1]
                    dve.wait_ge(low_ready[before], k_before + 1)
                transform(q, k)
                if q + 1 < LEAD:
                    dve.wait_ge(v_ready, q + 1)
                    differences(q + 1, (q + 1) % 2, PROLOGUE[q + 1][1])
                low(q, t, k)

            def body(m, last=False):
                for par in (0, 1):
                    final = last and par == 1
                    p = 2 * m + par + 1
                    for j in range(STEPS):
                        k = 8 * m + 4 * par + j
                        for t in (A, B, R):
                            g_par = (j + t) % 2
                            q, q_par = LEAD + 3 * k + t, (LEAD + j + t) % 2
                            ahead = {A: 1, B: 1, R: 2}[t]
                            jj = (j + ahead) % STEPS
                            prepares = not (final and j + ahead >= STEPS)
                            form_halves(k, t, g_par, j)
                            if prepares:
                                differences(q, q_par, jj)
                            if not final and (j, t) == (2, B):
                                group_inverse(p)
                            combine(k, t, g_par, j, (0,))
                            if prepares:
                                transform(q, jj)
                            combine(k, t, g_par, j, (1, 2, 3))
                            if not final and (j, t) == (1, R):
                                group_means(p)
                            if not final and (j, t) == (2, A):
                                group_variances(p)
                            add_x(k, t, par, j)
                            if prepares:
                                low(q, t, jj)
                            finish(k, t, g_par, par, j)

            with dve.Fori(0, PAIRS // 2 - 1) as m:
                body(m)
            body(PAIRS // 2 - 1, last=True)


def kernel(x, L0_conv_weight, L0_conv_bias):
    import concourse.bacc as bacc
    from concourse.bass_utils import run_bass_kernel_spmd

    weight = np.ascontiguousarray(L0_conv_weight)
    arrays = {
        "x": np.ascontiguousarray(x),
        "w_rows": weight,
        "w_cols": np.ascontiguousarray(weight.reshape(CH, CH, 3, KX).transpose(1, 2, 3, 0)),
        "bias": np.ascontiguousarray(L0_conv_bias).reshape(CH, 1),
        "matrices": group_matrices(),
        "identity": np.eye(P, dtype=np.float32),
    }
    nc = bacc.Bacc("TRN2", target_bir_lowering=False, num_devices=1)
    args = [nc.dram_tensor(name, a.shape, F32, kind="ExternalInput").ap() for name, a in arrays.items()]
    out = nc.dram_tensor("out", (IMAGES, CH, H, W), F32, kind="ExternalOutput").ap()
    preact_conv(nc, *args, out)
    r = run_bass_kernel_spmd(nc, [arrays], core_ids=[0])
    return r.results[0]["out"]
```
